# Optimizing a Trainium2 kernel written in Bass

```python
import numpy as np
import jax
import jax.numpy as jnp

def _softmax(x, axis=-1):
    return jax.nn.softmax(x, axis=axis)

def _gelu(x):
    return jax.nn.gelu(x, approximate=True)

def _silu(x):
    return jax.nn.silu(x)

def _sigmoid(x):
    return jax.nn.sigmoid(x)

def _layernorm(x, axis=-1, eps=1e-05):
    m = jnp.mean(x, axis=axis, keepdims=True)
    v = jnp.var(x, axis=axis, keepdims=True)
    return (x - m) / jnp.sqrt(v + eps)

def _scatter_add(tgt, idx, src, axis=0):
    return tgt.at[idx].add(src)

def _segment_sum(src, seg, n):
    return jax.ops.segment_sum(src, seg, n)
kernel_name = 'mk_flamingo_gated_d1_seqx_r8_f29c62'

def setup_inputs(seed: int=0):
    np.random.seed(seed)
    _w = jnp.asarray

    def _rec_inputs():
        import jax
        import jax.numpy as jnp
        _rk = jax.random.key(seed)
        x = -0.0003929 + 0.9999 * jax.random.normal(jax.random.fold_in(_rk, 1), (16, 128, 128), jnp.float32)
        _lenS = 128 - jax.random.randint(jax.random.fold_in(_rk, 7), (16,), 0, max(1, 128 // 4) + 1, jnp.int32)
        _lenS2 = 77 - jax.random.randint(jax.random.fold_in(_rk, 8), (16,), 0, max(1, 77 // 4) + 1, jnp.int32)
        _ctx_1024P = jax.random.normal(jax.random.fold_in(_rk, 11), (16, 16, 128), jnp.float32)
        _ctx_1024c = jax.random.dirichlet(jax.random.fold_in(_rk, 511), 0.3 * jnp.ones((16,), jnp.float32), (16, 77))
        _ctx_1024t = jnp.einsum('bsk,bkd->bsd', _ctx_1024c, _ctx_1024P)
        _ctx_1024t = _ctx_1024t * jax.lax.rsqrt(jnp.mean(jnp.square(_ctx_1024t)) + 1e-12) * 0.953939
        ctx_1024 = -1.39393e-06 + 0.999914 * (_ctx_1024t + 0.3 * jax.random.normal(jax.random.fold_in(_rk, 611), (16, 77, 128), jnp.float32))
        _g = jax.random.normal(jax.random.fold_in(_rk, 9001), (2, 1), jnp.float32)
        _g = jnp.sign(_g) * jnp.maximum(jnp.abs(_g), 1.0) + (_g == 0) * 1.0
        g_xattn = _g[0]
        g_ffn = _g[1]
        return (x, ctx_1024, g_xattn, g_ffn)
    x, ctx_1024, g_xattn, g_ffn = _rec_inputs()

    def _L0_xattn_setup():
        import jax, jax.numpy as jnp
        import numpy as np
        HEADS = 16
        EPS = 1e-06

        def _rmsnorm(x, gamma):
            inv = jax.lax.rsqrt(jnp.mean(x * x, axis=-1, keepdims=True) + EPS)
            return x * inv * gamma
        key = jax.random.key(seed)
        ks = jax.random.split(key, 7)
        B, L, Lc, D, CTX = (4, 512, 128, 128, 128)
        hd = D // HEADS
        s = 1.0 / np.sqrt(D)
        return {'x': jax.random.normal(ks[0], (B, L, D), jnp.float32), 'ctx': jax.random.normal(ks[1], (B, Lc, CTX), jnp.float32), 'Wq': jax.random.normal(ks[2], (D, D), jnp.float32) * s, 'Wkv': jax.random.normal(ks[3], (CTX, 2 * D), jnp.float32) * s, 'Wproj': jax.random.normal(ks[4], (D, D), jnp.float32) * s, 'q_gamma': jnp.ones((hd,), jnp.float32), 'k_gamma': jnp.ones((hd,), jnp.float32)}
    _L0_xattn_all = _L0_xattn_setup()
    _L0_xattn_in = {k: v for k, v in _L0_xattn_all.items() if k in ('Wq', 'Wkv', 'Wproj', 'q_gamma', 'k_gamma')}
    del _L0_xattn_all

    def _L0_ffn_setup():
        import jax, jax.numpy as jnp
        import numpy as np
        D_MODEL = 128
        D_FF = 512
        NUM_EXPERTS = 8
        TOP_K = 2
        key = jax.random.key(seed)
        ks = jax.random.split(key, 9)
        s = 0.02
        x = jax.random.normal(ks[0], (2, 256, D_MODEL), dtype=jnp.float32)
        Wg = jax.random.normal(ks[1], (D_MODEL, NUM_EXPERTS), dtype=jnp.float32) * s
        bg = jnp.zeros((NUM_EXPERTS,), dtype=jnp.float32)
        W1 = jax.random.normal(ks[2], (NUM_EXPERTS, D_MODEL, D_FF), dtype=jnp.float32) * s
        b1 = jnp.zeros((NUM_EXPERTS, D_FF), dtype=jnp.float32)
        W3 = jax.random.normal(ks[3], (NUM_EXPERTS, D_MODEL, D_FF), dtype=jnp.float32) * s
        b3 = jnp.zeros((NUM_EXPERTS, D_FF), dtype=jnp.float32)
        W2 = jax.random.normal(ks[4], (NUM_EXPERTS, D_FF, D_MODEL), dtype=jnp.float32) * s
        b2 = jnp.zeros((NUM_EXPERTS, D_MODEL), dtype=jnp.float32)
        return {'x': x, 'Wg': Wg, 'bg': bg, 'W1': W1, 'b1': b1, 'W3': W3, 'b3': b3, 'W2': W2, 'b2': b2}
    _L0_ffn_all = _L0_ffn_setup()
    _L0_ffn_in = {k: v for k, v in _L0_ffn_all.items() if k in ('Wg', 'bg', 'W1', 'b1', 'W3', 'b3', 'W2', 'b2')}
    del _L0_ffn_all
    return {'x': x, 'ctx_1024': ctx_1024, 'g_xattn': g_xattn, 'g_ffn': g_ffn, 'L0_xattn_Wq': _L0_xattn_in['Wq'], 'L0_xattn_Wkv': _L0_xattn_in['Wkv'], 'L0_xattn_Wproj': _L0_xattn_in['Wproj'], 'L0_xattn_q_gamma': _L0_xattn_in['q_gamma'], 'L0_xattn_k_gamma': _L0_xattn_in['k_gamma'], 'L0_ffn_Wg': _L0_ffn_in['Wg'], 'L0_ffn_bg': _L0_ffn_in['bg'], 'L0_ffn_W1': _L0_ffn_in['W1'], 'L0_ffn_b1': _L0_ffn_in['b1'], 'L0_ffn_W3': _L0_ffn_in['W3'], 'L0_ffn_b3': _L0_ffn_in['b3'], 'L0_ffn_W2': _L0_ffn_in['W2'], 'L0_ffn_b2': _L0_ffn_in['b2']}

def reference(x, ctx_1024, g_xattn, g_ffn, L0_xattn_Wq, L0_xattn_Wkv, L0_xattn_Wproj, L0_xattn_q_gamma, L0_xattn_k_gamma, L0_ffn_Wg, L0_ffn_bg, L0_ffn_W1, L0_ffn_b1, L0_ffn_W3, L0_ffn_b3, L0_ffn_W2, L0_ffn_b2):
    import jax
    import jax.numpy as jnp

    def _L0_xattn_ref(x, ctx, Wq, Wkv, Wproj, q_gamma, k_gamma):
        import jax, jax.numpy as jnp
        import numpy as np
        HEADS = 16
        EPS = 1e-06

        def _rmsnorm(x, gamma):
            inv = jax.lax.rsqrt(jnp.mean(x * x, axis=-1, keepdims=True) + EPS)
            return x * inv * gamma
        B, L, D = x.shape
        Lc = ctx.shape[1]
        H = HEADS
        hd = D // H
        q = (x @ Wq).reshape(B, L, H, hd).transpose(0, 2, 1, 3)
        kv = (ctx @ Wkv).reshape(B, Lc, 2, H, hd).transpose(2, 0, 3, 1, 4)
        k, v = (kv[0], kv[1])
        q = _rmsnorm(q, q_gamma)
        k = _rmsnorm(k, k_gamma)
        scale = 1.0 / np.sqrt(hd)
        attn = jnp.einsum('bhld,bhmd->bhlm', q, k) * scale
        attn = jax.nn.softmax(attn, axis=-1)
        out = jnp.einsum('bhlm,bhmd->bhld', attn, v)
        out = out.transpose(0, 2, 1, 3).reshape(B, L, D)
        return out @ Wproj

    def _L0_ffn_ref(x, Wg, bg, W1, b1, W3, b3, W2, b2):
        import jax, jax.numpy as jnp
        import numpy as np
        D_MODEL = 128
        D_FF = 512
        NUM_EXPERTS = 8
        TOP_K = 2
        logits = x @ Wg + bg
        probs = jax.nn.softmax(logits, axis=-1)
        top_v, top_i = jax.lax.top_k(probs, TOP_K)
        top_v = top_v / (top_v.sum(axis=-1, keepdims=True) + 1e-06)
        onehot = jax.nn.one_hot(top_i, NUM_EXPERTS, dtype=x.dtype)
        combine = jnp.einsum('bsk,bske->bse', top_v, onehot)
        out = jnp.zeros_like(x)
        for e in range(NUM_EXPERTS):
            h = jax.nn.silu(x @ W1[e] + b1[e]) * (x @ W3[e] + b3[e])
            out = out + combine[..., e:e + 1] * (h @ W2[e] + b2[e])
        return out
    x = x + jnp.tanh(g_xattn[0]) * _L0_xattn_ref(_layernorm(x, axis=-1), ctx_1024, L0_xattn_Wq, L0_xattn_Wkv, L0_xattn_Wproj, L0_xattn_q_gamma, L0_xattn_k_gamma)
    x = x + jnp.tanh(g_ffn[0]) * _L0_ffn_ref(_layernorm(x, axis=-1), L0_ffn_Wg, L0_ffn_bg, L0_ffn_W1, L0_ffn_b1, L0_ffn_W3, L0_ffn_b3, L0_ffn_W2, L0_ffn_b2)
    return x

_drawn_inputs = setup_inputs


def setup_inputs(seed=0):
    import zlib

    import numpy as np

    out = dict(_drawn_inputs(seed))
    spreads = {'L0_xattn_q_gamma': (1.0, 0.2),
     'L0_xattn_k_gamma': (1.0, 0.562),
     'L0_ffn_bg': (0.0, 0.1),
     'L0_ffn_b1': (0.0, 0.8),
     'L0_ffn_b3': (0.0, 0.8),
     'L0_ffn_b2': (0.0, 0.532)}
    factors = {'L0_ffn_W1': 7.11, 'L0_ffn_W3': 7.109, 'L0_ffn_W2': 6.468}
    for name, (base, spread) in spreads.items():
        noise = np.random.default_rng([zlib.crc32(name.encode()), seed]).standard_normal(out[name].shape)
        drawn = base * np.exp(spread * noise) if base else spread * noise
        out[name] = jnp.asarray(drawn.astype(out[name].dtype))
    for name, factor in factors.items():
        out[name] = (out[name] * factor).astype(out[name].dtype)
    return out
```

```python
import concourse.bass as bass
from concourse import mybir
from concourse.alu_op_type import AluOpType as ALU
from contextlib import ExitStack

P = 128
NBATCH = 16
D = 128
HEADS = 16
HD = D // HEADS
KEYS = 77
FF = 512
EXPERTS = 8
CB = 4
CHUNKS = NBATCH // CB
CT = CB * P
FB = FF // P
UNITS = EXPERTS * FB
HG = 4
GROUPS = HEADS // HG
SLOT = 32
VW = HD + 1
VG = 8
VS = VG * VW
KVW = 2 * D
LN_EPS, RMS_EPS, TOP_EPS = 1e-5, 1e-6, 1e-6
MAGIC = 0x5F3759DF

ATTN = ["xT", "q", "cT", "kv0", "kv1", "qT", "kT"] + [f"kS{b}" for b in range(CB)]
ATTN += ["max0", "max1", "qS0", "sA0", "sB0"]
for _b in range(1, CB):
    ATTN += [f"qS{_b}", f"sA{_b}", f"pv{_b - 1}", f"sB{_b}"]
    ATTN += [f"max{_b + 1}"] if _b + 1 < CB else []
    ATTN += [f"oT{_b - 1}"]
ATTN += [f"pv{CB - 1}", f"oT{CB - 1}", "oTT", "proj"]
ROUTE = ["x2T", "gate", "wT", "b2"]
SPREAD = [f"w{e}" for e in range(EXPERTS)]
UNIT_GROUPS = {"max": range(4), "sA": range(0, 2), "sB": range(2, 4)}
MIX = {n: k for k, n in enumerate(n for n in ATTN + ROUTE + SPREAD if n[:-1] not in UNIT_GROUPS)}
NMIX = len(MIX)
SCORE = {}
for _n in ATTN:
    for _g in UNIT_GROUPS.get(_n[:-1], ()):
        SCORE[("max" if _n[:3] == "max" else "sc", int(_n[-1]), _g)] = len(SCORE)
NSCORE = len(SCORE) // 2
NLINK = 66


def build(nc, x, ctx_in, gx, gf, Wq, Wkv, Wproj, qg, kg, Wg, bg, W1, b1, W3, b3, W2, b2, consts, out):
    f32, f32r = mybir.dt.float32, mybir.dt.float32r
    i32, u32 = mybir.dt.int32, mybir.dt.uint32
    ACT, AX = mybir.ActivationFunctionType, mybir.AxisListType

    with ExitStack() as stack:
        def sb(name, shape, dt=f32):
            return stack.enter_context(nc.sbuf_tensor(name, shape, dt))

        def sem(name):
            return stack.enter_context(nc.semaphore(name))

        NCONST = consts.shape[1]
        cst = sb("cst", [P, NCONST])
        ident = cst[:, 0:P]
        hmask = cst[:, P:P + HG]
        iota = cst[:, P + HG:P + HG + EXPERTS]
        is_hi = cst[0:3 * EXPERTS, P + HG + EXPERTS:P + HG + EXPERTS + 1]
        is_lo = cst[0:3 * EXPERTS, P + HG + EXPERTS + 1:P + HG + EXPERTS + 2]
        sel_raw = cst[0:SLOT, P + HG + EXPERTS + 2:NCONST]
        sel = sb("sel", [SLOT, EXPERTS], f32r)
        acc = sb("acc", [P, CT])
        wq_raw, wp_raw, wkv_raw = acc[:, 0:D], acc[:, D:2 * D], acc[:, 2 * D:2 * D + KVW]
        wg_raw = sb("wg_raw", [D, EXPERTS])
        wq = sb("wq", [D, 2, D], f32r)
        wp = sb("wp", [D, 2, D], f32r)
        wkv = sb("wkv", [D, 2, KVW], f32r)
        wg = sb("wg", [D, 2, EXPERTS], f32r)
        EW = 3 * FF
        w_hi = sb("w_hi", [P, EXPERTS, EW], f32r)
        w_lo = sb("w_lo", [P, EXPERTS, EW], f32r)
        b1_sb, b3_sb = sb("b1_sb", [P, UNITS]), sb("b3_sb", [P, UNITS])
        bg_sb = sb("bg_sb", [P, EXPERTS])
        WR = 3 * EXPERTS
        b2_raw, b2_d = sb("b2_raw", [WR, D]), sb("b2_d", [WR, D])
        b2_hi, b2_s = sb("b2_hi", [WR, D], f32r), sb("b2_s", [WR, D], f32r)
        gates = sb("gates", [P, 2])
        gk = sb("gk", [KEYS, HD])
        gq = sb("gq", [KEYS, HD])

        xc = sb("xc", [P, CB, D])
        cc = sb("cc", [KEYS, CB, D])
        x1 = sb("x1", [P, 2 * CT])
        pad, one = sb("pad", [P, 1]), sb("one", [P, 1])
        stats = sb("stats", [P, CB, 6])
        mv = sb("mv", [P, CB, 2])
        xn = sb("xn", [P, CB, D])
        xh, xl = sb("xh", [D, CT], f32r), sb("xl", [D, CT], f32r)
        ch, cl = sb("ch", [D, CB * KEYS], f32r), sb("cl", [D, CB * KEYS], f32r)
        qr, sq = sb("qr", [P, CT]), xn[:, :, :].rearrange("p b d -> p (b d)")
        on = sb("on", [P, CB, D])
        kvr, ksq = sb("kvr", [KEYS, CB, KVW]), on[0:KEYS, :, :]
        NR = CB * HEADS
        ss = sb("ss", [P, 2 * NR])
        nt1, nt2, rinv = sb("nt1", [P, 2 * NR]), sb("nt2", [P, 2 * NR]), sb("rinv", [P, 2 * NR])
        qn, qhi = sb("qn", [P, CT]), sq.bitcast(f32r)
        kn, khi = sb("kn", [KEYS, CT]), on[0:KEYS, :, :].rearrange("p b d -> p (b d)").bitcast(f32r)
        q_st = sb("q_st", [P, CB, HEADS, SLOT])
        k_st = q_st[0:KEYS]
        qTh = sb("qTh", [D, CT], f32r)
        kT = qr[:, 0:CB * KEYS]
        k_bd = sb("k_bd", [D, CB, HG, KEYS], f32r)
        ksT = sb("ksT", [P, CB, GROUPS, KEYS], f32r)
        qsT = sb("qsT", [P, 2, GROUPS, P], f32r)
        probs = sb("probs", [KEYS, HG, GROUPS, P])
        va = sb("va", [KEYS, 1, 2, VG * (VS + VW)])
        oa = sb("oa", [VS, 2 * P])
        rden = sb("rden", [P, HEADS])
        oh, ol = xh, xl
        x2h, x2l = sb("x2h", [D, CT], f32r), sb("x2l", [D, CT], f32r)
        lg, ex, pr = sb("lg", [P, CB, EXPERTS]), sb("ex", [P, CB, EXPERTS]), sb("pr", [P, CB, EXPERTS])
        r4, s4 = sb("r4", [P, CB]), sb("s4", [P, CB])
        top = sb("top", [P, CB, 8])
        topi = sb("topi", [P, CB, 8], u32)
        topf = sb("topf", [P, CB, 8])
        e1, e2 = sb("e1", [P, CB, EXPERTS]), sb("e2", [P, CB, EXPERTS])
        chi = sb("chi", [P, CB, EXPERTS], f32r)
        c_st = sb("c_st", [P, CB, SLOT])
        cT = sb("cT", [SLOT, CT], f32r)
        cbc = sb("cbc", [P, 2, CT])
        arena = sb("arena", [P, 2 * EW])
        w_raw = arena[:, :].rearrange("p (k w) -> p k w", k=2)
        sil, hf, yt = (arena[:, k * 2 * CT:(k + 1) * 2 * CT].rearrange("p (k t) -> p k t", k=2) for k in range(3))
        outb = yt[:, 0, :]
        hh, hl = sb("hh", [P, 2, CT], f32r), sb("hl", [P, 2, CT], f32r)

        def bank(name):
            return stack.enter_context(nc.psum_tensor(name, [P, 512], f32))

        up, gt = [bank("up0"), bank("up1")], [bank("gt0"), bank("gt1")]
        y = bank("y")
        score = [bank("score0"), bank("score1")]
        mix = bank("mix")

        cst_in, small_in, bias_in = sem("cst_in"), sem("small_in"), sem("bias_in")
        w_in = [sem("w_in0"), sem("w_in1")]
        x_in, c_in, out_done = sem("x_in"), sem("c_in"), sem("out_done")
        small_hi, small_lo = sem("small_hi"), sem("small_lo")
        w_hi_done, w_lo_done = sem("w_hi_done"), sem("w_lo_done")
        init_done, tanh_done, b2_hi_done = sem("init_done"), sem("tanh_done"), sem("b2_hi_done")
        gk_done = sem("gk_done")
        link_s = sem("link_s")
        mix_full, mix_free = sem("mix_full"), sem("mix_free")
        score_full = sem("score_full")
        score_free = [sem("score_free0"), sem("score_free1")]
        xn_done, xh_done, ch_done = sem("xn_done"), sem("xh_done"), sem("ch_done")
        qsq_done, ksq_done = sem("qsq_done"), sem("ksq_done")
        qn_done, kn_done, qhi_done, khi_done = sem("qn_done"), sem("kn_done"), sem("qhi_done"), sem("khi_done")
        qdup_done, kdup_done, klo_done = sem("qdup_done"), sem("kdup_done"), sem("klo_done")
        kbd_done, va_done = sem("kbd_done"), sem("va_done")
        pv_half = sem("pv_half")
        shift_done, on_done, oh_done, x1_done = sem("shift_done"), sem("on_done"), sem("oh_done"), sem("x1_done")
        xn2_done, x2h_done = sem("xn2_done"), sem("x2h_done")
        lg_done, ex_done, cst_done = sem("lg_done"), sem("ex_done"), sem("cst_done")
        up_full, gt_full = sem("up_full"), sem("gt_full")
        sil_done, h_done, hh_done, hl_done = sem("sil_done"), sem("h_done"), sem("hh_done"), sem("hl_done")
        y_part, y_free, acc_done, f_full = sem("y_part"), sem("y_free"), sem("acc_done"), sem("f_full")

        block = stack.enter_context(nc.Block())

        def mix_at(c, name):
            return NMIX * c + MIX[name] + 1

        def mix_before(c, name):
            return NMIX * c + MIX[name]

        def score_at(c, kind, b, g):
            return len(SCORE) * c + SCORE[(kind, b, g)] + 1

        def score_bank(kind, b, g):
            return SCORE[(kind, b, g)] % 2

        def score_before(c, kind, b, g):
            return NSCORE * c + SCORE[(kind, b, g)] // 2

        def x1_chunk(c):
            return x1[:, bass.ds((c % 2) * CT, CT)]

        @block.sync
        def _(sp):
            sp.dma_start(cst[:, :], consts).then_inc(cst_in, 16)
            sp.dma_start(wq_raw[:, :], Wq).then_inc(small_in, 16)
            sp.dma_start(wkv_raw[:, :], Wkv).then_inc(small_in, 16)
            sp.dma_start(wp_raw[:, :], Wproj).then_inc(small_in, 16)
            sp.dma_start(wg_raw[:, :], Wg).then_inc(small_in, 16)
            sp.dma_start(gates[:, 0:1], gx.partition_broadcast(P)).then_inc(bias_in, 16)
            sp.dma_start(gates[:, 1:2], gf.partition_broadcast(P)).then_inc(bias_in, 16)
            sp.dma_start(gq[:, :], qg.partition_broadcast(KEYS)).then_inc(bias_in, 16)
            sp.dma_start(gk[:, :], kg.partition_broadcast(KEYS)).then_inc(bias_in, 16)
            sp.dma_start(bg_sb[:, :], bg.partition_broadcast(P)).then_inc(bias_in, 16)
            sp.dma_start(b1_sb[:, :], b1).then_inc(bias_in, 16)
            sp.dma_start(b3_sb[:, :], b3).then_inc(bias_in, 16)
            for k in range(3):
                sp.dma_start(b2_raw[EXPERTS * k:EXPERTS * (k + 1), :], b2).then_inc(bias_in, 16)
            for e in range(EXPERTS):
                if e >= 2:
                    sp.wait_ge(w_hi_done, e - 1)
                    sp.wait_ge(w_lo_done, e - 1)
                dst = w_raw[:, e % 2, :]
                sp.dma_start(dst[:, 0:FF], W1[e, :, :]).then_inc(w_in[e % 2], 16)
                sp.dma_start(dst[:, FF:2 * FF], W3[e, :, :]).then_inc(w_in[e % 2], 16)
                sp.dma_start(dst[:, 2 * FF:EW].rearrange("p (f d) -> p f d", f=FB),
                             W2[e, :, :].rearrange("(f p) d -> p f d", p=P)).then_inc(w_in[e % 2], 16)
            with sp.Fori(0, CHUNKS) as c:
                sp.wait_ge(x1_done, c)
                sp.dma_start(xc[:, :, :], x[bass.ds(c * CB, CB), :, :].rearrange("b p d -> p b d")).then_inc(x_in, 16)
                sp.wait_ge(ch_done, c)
                sp.dma_start(cc[:, :, :], ctx_in[bass.ds(c * CB, CB), :, :].rearrange("b p d -> p b d")).then_inc(c_in, 16)
                sp.wait_ge(y_free, (EXPERTS + 1) * c + EXPERTS + 1)
                sp.dma_start(out[bass.ds(c * CB, CB), :, :].rearrange("b p d -> p b d"),
                             outb.rearrange("p (b d) -> p b d", b=CB)).then_inc(out_done, 16)
            sp.wait_ge(out_done, 16 * CHUNKS)

        @block.gpsimd
        def _(pool):
            for e in range(EXPERTS):
                pool.wait_ge(w_hi_done, e + 1)
                nc.gpsimd.tensor_tensor(w_lo[:, e, :], w_raw[:, e % 2, :], w_hi[:, e, :].bitcast(f32),
                                        ALU.subtract).then_inc(w_lo_done, 1)
            pool.wait_ge(init_done, 4)

            def same(dst, src):
                ones = one[0:src.shape[0], :]
                while len(ones.shape) < len(src.shape):
                    ones = ones.unsqueeze(1)
                return nc.gpsimd.tensor_tensor(dst, src, ones.to_broadcast(list(src.shape)), ALU.mult)

            def attn(c):
                for b in range(CB):
                    if b == 0:
                        pool.wait_ge(khi_done, c + 1)
                        pool.wait_ge(mix_full, mix_at(c, "q"))
                    src = khi[:, b * D:(b + 1) * D].bitcast(f32).rearrange("p (h d) -> p h d", d=HD)
                    same(k_st[:, b, :, 0:HD], src).then_inc(kdup_done, 1)
                    same(k_st[:, b, :, HD:2 * HD], src).then_inc(kdup_done, 1)
                pool.wait_ge(qhi_done, c + 1)
                pool.wait_ge(mix_full, mix_at(c, "kS3"))
                for b in range(CB):
                    src = qhi[:, b * D:(b + 1) * D].bitcast(f32).rearrange("p (h d) -> p h d", d=HD)
                    same(q_st[:, b, :, 0:HD], src).then_inc(qdup_done, 1)
                    same(q_st[:, b, :, 2 * HD:3 * HD], src).then_inc(qdup_done, 1)
                pool.wait_ge(mix_free, mix_at(c, "kT"))
                for b in range(CB):
                    kb = kT[:, b * KEYS:(b + 1) * KEYS]
                    nc.gpsimd.tensor_tensor(
                        k_bd[:, b, :, :], kb.unsqueeze(1).to_broadcast([D, HG, KEYS]),
                        hmask.unsqueeze(2).to_broadcast([D, HG, KEYS]), ALU.mult).then_inc(kbd_done, 1)
                for b in range(CB):
                    if b >= 1:
                        pool.wait_ge(mix_full, mix_at(c, f"pv{b - 1}"))
                    for g in range(2):
                        src = kvr[:, b, D:2 * D].rearrange("p (i g j d) -> p i g j d", i=GROUPS, g=2, d=HD)[:, :, g]
                        dst = va[:, 0, g, :].rearrange("p (i j s) -> p i j s", i=GROUPS, j=2)[:, :, :, 0:HD]
                        same(dst, src).then_inc(va_done, 1)

            def ffn(c):
                for t in range(UNITS):
                    e, f = divmod(t, FB)
                    pool.wait_ge(hh_done, UNITS * c + t + 1)
                    if t >= 2:
                        pool.wait_ge(y_part, UNITS * c + t - 1)
                    nc.gpsimd.tensor_tensor(hl[:, t % 2, :], hf[:, t % 2, :], hh[:, t % 2, :].bitcast(f32),
                                            ALU.subtract).then_inc(hl_done, 1)
                    if t >= FB and f == 2:
                        add_y(c, e - 1)
                add_y(c, EXPERTS - 1)

            def add_y(c, e):
                pool.wait_ge(y_free, (EXPERTS + 1) * c + e + 1)
                pool.wait_ge(mix_free, mix_at(c, "b2"))
                pool.wait_ge(acc_done, EXPERTS * c + e)
                nc.gpsimd.tensor_tensor(acc[:, :], acc[:, :], yt[:, e % 2, :], ALU.add).then_inc(acc_done, 1)

            with pool.Fori(0, CHUNKS) as c:
                attn(c)
                ffn(c)

        @block.scalar
        def _(act):
            act.wait_ge(small_in, 64)
            nc.scalar.copy(wq[:, 0, :], wq_raw[:, :]).then_inc(small_hi, 1)
            nc.scalar.copy(wkv[:, 0, :], wkv_raw[:, :]).then_inc(small_hi, 1)
            nc.scalar.copy(wp[:, 0, :], wp_raw[:, :]).then_inc(small_hi, 1)
            nc.scalar.copy(wg[:, 0, :], wg_raw[:, :]).then_inc(small_hi, 1)
            act.wait_ge(cst_in, 16)
            nc.scalar.copy(sel[:, :], sel_raw).then_inc(small_hi, 1)
            act.wait_ge(bias_in, 160)
            nc.scalar.activation(gates[:, :], gates[:, :], ACT.Tanh).then_inc(tanh_done, 1)
            nc.scalar.copy(b2_hi[:, :], b2_raw[:, :]).then_inc(b2_hi_done, 1)
            for e in range(EXPERTS):
                act.wait_ge(w_in[e % 2], 48 * (e // 2 + 1))
                nc.scalar.copy(w_hi[:, e, :], w_raw[:, e % 2, :]).then_inc(w_hi_done, 1)

            def attn(c):
                for n in ATTN:
                    if n[:3] == "max":
                        continue
                    if n[:2] in ("sA", "sB"):
                        b = int(n[2:])
                        for j in UNIT_GROUPS[n[:2]]:
                            k = score_bank("sc", b, j)
                            act.wait_ge(score_full, score_at(c, "sc", b, j))
                            if b >= 1 and j == 0:
                                act.wait_ge(pv_half, CB * c + b)
                            if b >= 1 and j == 2:
                                act.wait_ge(mix_full, mix_at(c, f"pv{b - 1}"))
                            nc.scalar.activation(probs[:, j, :, :].rearrange("p i t -> p (i t)"),
                                                 score[k][0:KEYS, :], ACT.Exp).then_inc(score_free[k], 1)
                        continue
                    act.wait_ge(mix_full, mix_at(c, n))
                    if n == "xT":
                        nc.scalar.copy(xh[:, :], mix[:, :]).then_inc(xh_done, 1)
                    elif n == "q":
                        nc.scalar.activation(sq[:, :], mix[:, :], ACT.Square).then_inc(qsq_done, 1)
                        nc.scalar.copy(qr[:, :], mix[:, :]).then_inc(mix_free, 1)
                    elif n == "cT":
                        nc.scalar.copy(ch[:, :], mix[:, 0:CB * KEYS]).then_inc(ch_done, 1)
                    elif n[:2] == "kv":
                        a = 2 * int(n[2:])
                        src = mix[0:KEYS, :].rearrange("p (b w) -> p b w", b=2)
                        nc.scalar.activation(ksq[:, a:a + 2, :], src[:, :, 0:D], ACT.Square).then_inc(ksq_done, 1)
                        nc.scalar.copy(kvr[:, a:a + 2, :], src).then_inc(mix_free, 1)
                    elif n == "qT":
                        nc.scalar.copy(qTh[:, :], mix[:, :]).then_inc(mix_free, 1)
                    elif n == "kT":
                        nc.scalar.copy(kT[:, :], mix[:, 0:CB * KEYS]).then_inc(mix_free, 1)
                    elif n[:2] == "kS":
                        b = int(n[2:])
                        nc.scalar.copy(ksT[:, b, :, :].rearrange("p i t -> p (i t)"),
                                       mix[:, 0:GROUPS * KEYS]).then_inc(mix_free, 1)
                    elif n[:2] == "qS":
                        b = int(n[2:])
                        nc.scalar.copy(qsT[:, b % 2, :, :].rearrange("p i t -> p (i t)"),
                                       mix[:, :]).then_inc(mix_free, 1)
                    elif n[:2] == "pv":
                        nc.scalar.copy(oa[:, :], mix[0:VS, 0:2 * P]).then_inc(mix_free, 1)
                    elif n == "oTT":
                        nc.scalar.copy(oh[:, :], mix[:, :]).then_inc(oh_done, 1)

            def route(c):
                act.wait_ge(mix_full, mix_at(c, "x2T"))
                act.wait_ge(gt_full, UNITS * c)
                nc.scalar.copy(x2h[:, :], mix[:, :]).then_inc(x2h_done, 1)
                act.wait_ge(lg_done, c + 1)
                nc.scalar.activation(ex[:, :, :], lg[:, :, :], ACT.Exp).then_inc(ex_done, 1)
                act.wait_ge(mix_full, mix_at(c, "wT"))
                nc.scalar.copy(cT[:, :], mix[0:SLOT, :]).then_inc(mix_free, 1)
                act.wait_ge(mix_full, mix_at(c, "b2"))
                act.wait_ge(f_full, c)
                nc.scalar.copy(acc[:, :], mix[:, :]).then_inc(mix_free, 1)

            def spread(c, e):
                act.wait_ge(mix_full, mix_at(c, f"w{e}"))
                if e >= 2:
                    act.wait_ge(y_free, (EXPERTS + 1) * c + e - 1)
                nc.scalar.copy(cbc[:, e % 2, :], mix[:, :]).then_inc(mix_free, 1)

            def ffn(c):
                for t in range(UNITS + 1):
                    if t % FB == 1:
                        spread(c, t // FB)
                    if t < UNITS:
                        act.wait_ge(up_full, UNITS * c + t + 1)
                        if t >= 2:
                            act.wait_ge(h_done, UNITS * c + t - 1)
                        nc.scalar.activation(sil[:, t % 2, :], up[t % 2][:, :], ACT.Silu,
                                             bias=b1_sb[:, t:t + 1]).then_inc(sil_done, 1)
                    if t >= 1:
                        u = t - 1
                        act.wait_ge(h_done, UNITS * c + u + 1)
                        if u >= 2:
                            act.wait_ge(y_part, UNITS * c + u - 1)
                        nc.scalar.copy(hh[:, u % 2, :], hf[:, u % 2, :]).then_inc(hh_done, 1)

            with act.Fori(0, CHUNKS) as c:
                attn(c)
                route(c)
                ffn(c)

        @block.vector
        def _(dve):
            ve = nc.vector
            ve.memset(q_st[:, :, :, :], 0.0).then_inc(init_done, 1)
            ve.memset(c_st[:, :, :], 0.0).then_inc(init_done, 1)
            ve.memset(va[:, :, :, :], 0.0).then_inc(init_done, 1)
            dve.wait_ge(init_done, 3)
            for g in range(2):
                ve.memset(va[:, 0, g, :].rearrange("p (h s) -> p h s", h=VG)[:, :, HD:HD + 1], 1.0)
            ve.memset(one[:, :], 1.0)
            ve.memset(ss[:, :], 1.0).then_inc(init_done, 1)
            dve.wait_ge(bias_in, 160)
            dve.wait_ge(cst_in, 16)
            dve.wait_ge(init_done, 4)
            ve.scalar_tensor_tensor(out=gk[:, :], in0=gk[:, :], scalar=float(HD) ** -0.5, in1=gq[:, :],
                                    op0=ALU.mult, op1=ALU.mult).then_inc(gk_done, 1)
            dve.wait_ge(b2_hi_done, 1)
            ve.tensor_tensor(b2_d[:, :], b2_raw[:, :], b2_hi[:, :].bitcast(f32), ALU.subtract).then_inc(gk_done, 1)
            dve.wait_ge(gk_done, 2)
            ve.tensor_scalar(b2_raw[:, :], b2_hi[:, :].bitcast(f32), is_hi, None, ALU.mult).then_inc(gk_done, 1)
            dve.wait_ge(gk_done, 3)
            ve.scalar_tensor_tensor(out=b2_s[:, :], in0=b2_d[:, :], scalar=is_lo, in1=b2_raw[:, :],
                                    op0=ALU.mult, op1=ALU.add).then_inc(gk_done, 1)
            for k, (raw, hi, lo) in enumerate([(wq_raw[:, :], wq[:, 0, :], wq[:, 1, :]),
                                               (wkv_raw[:, :], wkv[:, 0, :], wkv[:, 1, :]),
                                               (wp_raw[:, :], wp[:, 0, :], wp[:, 1, :]),
                                               (wg_raw[:, :], wg[:, 0, :], wg[:, 1, :])]):
                dve.wait_ge(small_hi, k + 1)
                ve.tensor_tensor(lo, raw, hi.bitcast(f32), ALU.subtract).then_inc(small_lo, 1)

            links = [0]

            def link(c, ins):
                links[0] += 1
                ins.then_inc(link_s, 1)
                dve.wait_ge(link_s, NLINK * c + links[0])

            def inv_sqrt(c, v, dst, t1, t2):
                link(c, ve.tensor_scalar(t1.bitcast(i32), v.bitcast(i32), 1, None, ALU.logical_shift_right))
                link(c, ve.tensor_scalar(dst.bitcast(i32), t1.bitcast(i32), -1.0, float(MAGIC), ALU.mult, ALU.add))
                link(c, ve.tensor_scalar(v, v, -0.5, None, ALU.mult))
                for _ in range(3):
                    link(c, ve.tensor_tensor(t1, dst, dst, ALU.mult))
                    link(c, ve.tensor_tensor(t2, t1, v, ALU.mult))
                    link(c, ve.scalar_tensor_tensor(out=dst, in0=t2, scalar=1.5, in1=dst,
                                                    op0=ALU.add, op1=ALU.mult))

            def hold():
                return ve.memset(pad[:, :], 0.0)

            def norm(c, src, dst_done, last_read):
                for b in range(CB):
                    ins = ve.bn_stats(stats[:, b, :], src[:, b, :])
                link(c, ins)
                hold()
                for b in range(CB):
                    ins = ve.bn_aggr(mv[:, b, :], stats[:, b, :])
                link(c, ins)
                link(c, ve.tensor_scalar(s4[:, :], mv[:, :, 1], LN_EPS, None, ALU.add))
                inv_sqrt(c, s4[:, :], r4[:, :], nt1[:, 0:CB], nt2[:, 0:CB])
                dve.wait_ge(mix_full, last_read)
                for b in range(CB):
                    ins = ve.tensor_scalar(xn[:, b, :], src[:, b, :], mv[:, b, 0:1], r4[:, b:b + 1],
                                           ALU.subtract, ALU.mult)
                ins.then_inc(dst_done, 1)

            def heads(ap):
                return ap.rearrange("p (h d) -> p h d", d=HD)

            def attn(c):
                ve.memset(k_st[:, :, :, 3 * HD:3 * HD + 1], 1.0)
                dve.wait_ge(x_in, 16 * c + 16)
                hold()
                norm(c, xc, xn_done, NMIX * c)
                dve.wait_ge(xh_done, c + 1)
                ve.tensor_tensor(xl[:, :], mix[:, :], xh[:, :].bitcast(f32), ALU.subtract).then_inc(mix_free, 1)
                dve.wait_ge(qsq_done, c + 1)
                ve.tensor_reduce(ss[:, 0:NR], heads(sq[:, :]), AX.X, ALU.add)
                dve.wait_ge(ch_done, c + 1)
                ve.tensor_tensor(cl[:, :], mix[:, 0:CB * KEYS], ch[:, :].bitcast(f32),
                                 ALU.subtract).then_inc(mix_free, 1)
                dve.wait_ge(ksq_done, 2 * c + 2)
                link(c, ve.tensor_reduce(ss[0:KEYS, NR:2 * NR],
                                         heads(ksq[:, :, :].rearrange("p b d -> p (b d)")), AX.X, ALU.add))
                link(c, ve.tensor_scalar(ss[:, :], ss[:, :], 1.0 / HD, RMS_EPS, ALU.mult, ALU.add))
                inv_sqrt(c, ss[:, :], rinv[:, :], nt1[:, :], nt2[:, :])
                dve.wait_ge(mix_free, mix_at(c, "kv1"))
                rk = rinv[0:KEYS, NR:2 * NR]
                for b in range(CB):
                    ins = ve.tensor_tensor(heads(kn[:, b * D:(b + 1) * D]), heads(kvr[:, b, 0:D]),
                                           rk[:, b * HEADS:(b + 1) * HEADS].unsqueeze(2)
                                           .to_broadcast([KEYS, HEADS, HD]), ALU.mult)
                link(c, ins)
                ve.tensor_tensor(heads(kn[:, :]), heads(kn[:, :]),
                                 gk[:, :].unsqueeze(1).to_broadcast([KEYS, NR, HD]), ALU.mult).then_inc(kn_done, 1)
                ve.tensor_tensor(heads(qn[:, :]), heads(qr[:, :]),
                                 rinv[:, 0:NR].unsqueeze(2).to_broadcast([P, NR, HD]), ALU.mult).then_inc(qn_done, 1)
                dve.wait_ge(kn_done, c + 1)
                ve.tensor_copy(khi[:, :], kn[:, :]).then_inc(khi_done, 1)
                dve.wait_ge(qn_done, c + 1)
                ve.tensor_copy(qhi[:, :], qn[:, :]).then_inc(qhi_done, 1)
                dve.wait_ge(khi_done, c + 1)
                for b in range(CB):
                    ve.tensor_tensor(k_st[:, b, :, 2 * HD:3 * HD], heads(kn[:, b * D:(b + 1) * D]),
                                     heads(khi[:, b * D:(b + 1) * D].bitcast(f32)),
                                     ALU.subtract).then_inc(klo_done, 1)
                dve.wait_ge(qhi_done, c + 1)
                dve.wait_ge(mix_full, mix_at(c, "kS3"))
                for b in range(CB):
                    ve.tensor_tensor(q_st[:, b, :, HD:2 * HD], heads(qn[:, b * D:(b + 1) * D]),
                                     heads(qhi[:, b * D:(b + 1) * D].bitcast(f32)),
                                     ALU.subtract)
                for n in ATTN:
                    if n[:3] == "max":
                        b = int(n[3:])
                        for g in range(GROUPS):
                            k = score_bank("max", b, g)
                            dve.wait_ge(score_full, score_at(c, "max", b, g))
                            src = score[k][:, 0:HG * KEYS].rearrange("p (h t) -> p h t", h=HG)
                            ve.tensor_reduce(q_st[:, b, HG * g:HG * (g + 1), 3 * HD], src, AX.X, ALU.max,
                                             negate=True).then_inc(score_free[k], 1)
                    elif n[:2] == "oT" and n != "oTT":
                        b = int(n[2:])
                        dve.wait_ge(mix_full, mix_at(c, n))
                        o = mix[:, 0:2 * VS].rearrange("p (h s) -> p h s", s=VW)
                        link(c, ve.reciprocal(rden[:, :], o[:, :, HD]))
                        for g in range(2):
                            ins = ve.tensor_tensor(
                                on[:, b, :].rearrange("p (i g j d) -> p i g j d", i=GROUPS, g=2, d=HD)[:, :, g],
                                o[:, g * VG:(g + 1) * VG, 0:HD].rearrange("p (i j) d -> p i j d", j=2),
                                rden[:, g * VG:(g + 1) * VG].rearrange("p (i j) -> p i j", j=2)
                                .unsqueeze(3).to_broadcast([P, GROUPS, 2, HD]), ALU.mult)
                        ins.then_inc(mix_free, 1)
                dve.wait_ge(oh_done, c + 1)
                ve.tensor_tensor(ol[:, :], mix[:, :], oh[:, :].bitcast(f32), ALU.subtract).then_inc(mix_free, 1)
                dve.wait_ge(mix_full, mix_at(c, "proj"))
                dve.wait_ge(tanh_done, 1)
                ve.scalar_tensor_tensor(out=x1_chunk(c), in0=mix[:, :], scalar=gates[:, 0:1],
                                        in1=xc[:, :, :].rearrange("p b d -> p (b d)"),
                                        op0=ALU.mult, op1=ALU.add).then_inc(mix_free, 1)

            def route(c):
                dve.wait_ge(mix_free, mix_at(c, "proj"))
                hold().then_inc(x1_done, 1)
                norm(c, x1_chunk(c).rearrange("p (b d) -> p b d", b=CB), xn2_done, mix_at(c, "xT"))
                dve.wait_ge(x2h_done, c + 1)
                ve.tensor_tensor(x2l[:, :], mix[:, :], x2h[:, :].bitcast(f32), ALU.subtract).then_inc(mix_free, 1)
                dve.wait_ge(mix_full, mix_at(c, "gate"))
                ve.tensor_tensor(lg[:, :, :], mix[:, 0:CB * EXPERTS].rearrange("p (b e) -> p b e", b=CB),
                                 bg_sb[:, :].unsqueeze(1).to_broadcast([P, CB, EXPERTS]),
                                 ALU.add).then_inc(mix_free, 1)
                dve.wait_ge(mix_free, mix_at(c, "gate"))
                link(c, ve.tensor_reduce(r4[:, :], lg[:, :, :], AX.X, ALU.max))
                ve.tensor_tensor(lg[:, :, :], lg[:, :, :], r4[:, :].unsqueeze(2).to_broadcast([P, CB, EXPERTS]),
                                 ALU.subtract).then_inc(lg_done, 1)
                dve.wait_ge(ex_done, c + 1)
                link(c, ve.tensor_reduce(s4[:, :], ex[:, :, :], AX.X, ALU.add))
                link(c, ve.reciprocal(r4[:, :], s4[:, :]))
                link(c, ve.tensor_tensor(pr[:, :, :], ex[:, :, :],
                                         r4[:, :].unsqueeze(2).to_broadcast([P, CB, EXPERTS]), ALU.mult))
                hold()
                for b in range(CB):
                    ins = ve.max(top[:, b, :], pr[:, b, :])
                link(c, ins)
                hold()
                for b in range(CB):
                    ins = ve.max_index(topi[:, b, :], top[:, b, :], pr[:, b, :])
                link(c, ins)
                link(c, ve.tensor_copy(topf[:, :, 0:2], topi[:, :, 0:2]))
                link(c, ve.tensor_tensor(s4[:, :], top[:, :, 0], top[:, :, 1], ALU.add))
                link(c, ve.tensor_scalar(s4[:, :], s4[:, :], TOP_EPS, None, ALU.add))
                link(c, ve.reciprocal(r4[:, :], s4[:, :]))
                link(c, ve.tensor_tensor(top[:, :, 0:2], top[:, :, 0:2],
                                         r4[:, :].unsqueeze(2).to_broadcast([P, CB, 2]), ALU.mult))
                io = iota.unsqueeze(1).to_broadcast([P, CB, EXPERTS])
                for k, e in enumerate((e1, e2)):
                    link(c, ve.tensor_tensor(e[:, :, :], io, topf[:, :, k:k + 1].to_broadcast([P, CB, EXPERTS]),
                                             ALU.is_equal))
                    link(c, ve.tensor_tensor(e[:, :, :], e[:, :, :],
                                             top[:, :, k:k + 1].to_broadcast([P, CB, EXPERTS]), ALU.mult))
                link(c, ve.tensor_tensor(e1[:, :, :], e1[:, :, :], e2[:, :, :], ALU.add))
                link(c, ve.tensor_copy(chi[:, :, :], e1[:, :, :]))
                ve.tensor_copy(c_st[:, :, 0:EXPERTS], chi[:, :, :].bitcast(f32))
                ve.tensor_copy(c_st[:, :, 2 * EXPERTS:3 * EXPERTS], chi[:, :, :].bitcast(f32))
                ve.tensor_tensor(c_st[:, :, EXPERTS:2 * EXPERTS], e1[:, :, :], chi[:, :, :].bitcast(f32),
                                 ALU.subtract).then_inc(cst_done, 1)

            def weigh_y(c, e):
                dve.wait_ge(y_part, UNITS * c + FB * (e + 1))
                dve.wait_ge(mix_free, mix_at(c, f"w{e}"))
                if e == 0:
                    dve.wait_ge(out_done, 16 * c)
                if e >= 2:
                    dve.wait_ge(acc_done, EXPERTS * c + e - 1)
                ve.tensor_tensor(yt[:, e % 2, :], y[:, :], cbc[:, e % 2, :], ALU.mult).then_inc(y_free, 1)

            def ffn(c):
                for t in range(UNITS):
                    e, f = divmod(t, FB)
                    dve.wait_ge(gt_full, UNITS * c + t + 1)
                    dve.wait_ge(sil_done, UNITS * c + t + 1)
                    if t >= 2:
                        dve.wait_ge(hl_done, UNITS * c + t - 1)
                    ve.scalar_tensor_tensor(out=hf[:, t % 2, :], in0=gt[t % 2][:, :], scalar=b3_sb[:, t:t + 1],
                                            in1=sil[:, t % 2, :], op0=ALU.add, op1=ALU.mult).then_inc(h_done, 1)
                    if t >= FB and f == 2:
                        weigh_y(c, e - 1)
                weigh_y(c, EXPERTS - 1)
                dve.wait_ge(f_full, c + 1)
                ve.scalar_tensor_tensor(out=outb, in0=y[:, :], scalar=gates[:, 1:2], in1=x1_chunk(c),
                                        op0=ALU.mult, op1=ALU.add).then_inc(y_free, 1)

            with dve.Fori(0, CHUNKS) as c:
                attn(c)
                route(c)
                ffn(c)
            assert links[0] == NLINK, links[0]

        @block.tensor
        def _(pe):
            pe.wait_ge(cst_in, 16)
            pe.wait_ge(small_hi, 5)
            pe.wait_ge(small_lo, 4)

            def three(dst, a_hi, a_lo, b_hi, b_lo, start=True, stop=True):
                nc.tensor.matmul(dst, a_hi, b_hi, start=start, stop=False)
                nc.tensor.matmul(dst, a_lo, b_hi, start=False, stop=False)
                return nc.tensor.matmul(dst, a_hi, b_lo, start=False, stop=stop)

            def turn(dst, src, n):
                return nc.tensor.transpose(dst, src, ident[0:n, 0:n])

            def attn(c):
                for n in ATTN:
                    if n[:-1] in UNIT_GROUPS:
                        kind, b = "max" if n[:3] == "max" else "sc", int(n[-1])
                        if kind == "max" and b == 0:
                            pe.wait_ge(kbd_done, CB * c + CB)
                        if n[:2] == "sA":
                            pe.wait_ge(mix_free, mix_at(c, f"qS{b}"))
                        for g in UNIT_GROUPS[n[:-1]]:
                            k = score_bank(kind, b, g)
                            pe.wait_ge(score_free[k], score_before(c, kind, b, g))
                            r = slice(SLOT * g, SLOT * (g + 1))
                            if kind == "max":
                                last = nc.tensor.matmul(score[k][:, 0:HG * KEYS], qTh[r, b * P:(b + 1) * P],
                                                        k_bd[r, b, :, :].rearrange("p h t -> p (h t)"),
                                                        start=True, stop=True)
                            else:
                                for i in range(GROUPS):
                                    last = nc.tensor.matmul(score[k][0:KEYS, i * P:(i + 1) * P],
                                                            ksT[r, b, i, :], qsT[r, b % 2, i, :],
                                                            start=True, stop=True)
                            last.then_inc(score_full, 1)
                        continue
                    if n == "xT":
                        pe.wait_ge(xn_done, c + 1)
                    elif n == "cT":
                        pe.wait_ge(c_in, 16 * c + 16)
                    elif n == "kT":
                        pe.wait_ge(kn_done, c + 1)
                    elif n == "qT":
                        pe.wait_ge(qn_done, c + 1)
                    elif n[:2] == "kS":
                        pe.wait_ge(kdup_done, 2 * CB * c + 2 * (int(n[2:]) + 1))
                        pe.wait_ge(klo_done, CB * c + int(n[2:]) + 1)
                    elif n[:2] == "qS":
                        b = int(n[2:])
                        pe.wait_ge(qdup_done, 2 * CB * c + 2 * (b + 1))
                        for g in (2, 3):
                            pe.wait_ge(score_free[score_bank("max", b, g)], score_before(c, "max", b, g) + 1)
                    elif n[:2] == "pv":
                        b = int(n[2:])
                        for g in (2, 3):
                            pe.wait_ge(score_free[score_bank("sc", b, g)], score_before(c, "sc", b, g) + 1)
                        pe.wait_ge(va_done, 2 * CB * c + 2 * (b + 1))
                    pe.wait_ge(mix_free, mix_before(c, n))
                    if n == "xT":
                        for b in range(CB):
                            last = turn(mix[:, b * P:(b + 1) * P], xn[:, b, :], P)
                    elif n == "q":
                        for b in range(CB):
                            s = slice(b * P, (b + 1) * P)
                            last = three(mix[:, s], xh[:, s], xl[:, s], wq[:, 0, :], wq[:, 1, :])
                    elif n == "cT":
                        for b in range(CB):
                            last = turn(mix[:, b * KEYS:(b + 1) * KEYS], cc[:, b, :], KEYS)
                    elif n[:2] == "kv":
                        for k in range(2):
                            s = slice((2 * int(n[2:]) + k) * KEYS, (2 * int(n[2:]) + k + 1) * KEYS)
                            last = three(mix[0:KEYS, k * KVW:(k + 1) * KVW], ch[:, s], cl[:, s],
                                         wkv[:, 0, :], wkv[:, 1, :])
                    elif n == "qT":
                        for b in range(CB):
                            last = turn(mix[:, b * P:(b + 1) * P], qn[:, b * D:(b + 1) * D], P)
                    elif n == "kT":
                        for b in range(CB):
                            last = turn(mix[:, b * KEYS:(b + 1) * KEYS], kn[:, b * D:(b + 1) * D], KEYS)
                    elif n[:2] == "kS":
                        for i in range(GROUPS):
                            src = k_st[:, int(n[2:]), HG * i:HG * (i + 1), :].rearrange("p h s -> p (h s)")
                            last = turn(mix[:, i * KEYS:(i + 1) * KEYS], src, KEYS)
                    elif n[:2] == "qS":
                        for i in range(GROUPS):
                            src = q_st[:, int(n[2:]), HG * i:HG * (i + 1), :].rearrange("p h s -> p (h s)")
                            last = turn(mix[:, i * P:(i + 1) * P], src, P)
                    elif n[:2] == "pv":
                        b = int(n[2:])
                        for g in range(2):
                            for h in range(VG):
                                i, j = h // 2, 2 * g + h % 2
                                last = nc.tensor.matmul(mix[0:VS, g * P:(g + 1) * P],
                                                        va[:, 0, g, h * VS:(h + 1) * VS],
                                                        probs[:, j, i, :], start=(h == 0), stop=(h == VG - 1))
                            if g == 0:
                                last.then_inc(pv_half, 1)
                    elif n == "oTT":
                        for b in range(CB):
                            last = turn(mix[:, b * P:(b + 1) * P], on[:, b, :], P)
                    elif n[:2] == "oT":
                        for g in range(2):
                            last = turn(mix[:, g * VS:(g + 1) * VS], oa[:, g * P:(g + 1) * P], VS)
                    elif n == "proj":
                        for b in range(CB):
                            s = slice(b * P, (b + 1) * P)
                            last = three(mix[:, s], oh[:, s], ol[:, s], wp[:, 0, :], wp[:, 1, :])
                    last.then_inc(mix_full, 1)

            def route(c):
                for n in ROUTE:
                    if n == "x2T":
                        pe.wait_ge(xn2_done, c + 1)
                    elif n == "wT":
                        pe.wait_ge(cst_done, c + 1)
                    elif n == "b2":
                        pe.wait_ge(gk_done, 4)
                    pe.wait_ge(mix_free, mix_before(c, n))
                    if n == "x2T":
                        for b in range(CB):
                            last = turn(mix[:, b * P:(b + 1) * P], xn[:, b, :], P)
                    elif n == "gate":
                        for b in range(CB):
                            s = slice(b * P, (b + 1) * P)
                            last = three(mix[:, b * EXPERTS:(b + 1) * EXPERTS], x2h[:, s], x2l[:, s],
                                         wg[:, 0, :], wg[:, 1, :])
                    elif n == "wT":
                        for b in range(CB):
                            last = turn(mix[0:SLOT, b * P:(b + 1) * P], c_st[:, b, :], P)
                    if n == "b2":
                        last = nc.tensor.matmul(mix[:, :], b2_s[:, :], cT[0:WR, :], start=True, stop=True)
                    last.then_inc(mix_full, 1)

            def ffn(c):
                LAG = 2
                for t in range(UNITS + LAG):
                    if t < UNITS and t % FB == 0:
                        e = t // FB
                        pe.wait_ge(mix_free, mix_before(c, f"w{e}"))
                        nc.tensor.matmul(mix[:, :], sel[0:16, e:e + 1].to_broadcast([16, P]), cT[0:16, :],
                                         start=True, stop=True).then_inc(mix_full, 1)
                    if t < UNITS:
                        e, f = divmod(t, FB)
                        for k, (bank_, full, free) in enumerate([(up[t % 2], up_full, sil_done),
                                                                 (gt[t % 2], gt_full, h_done)]):
                            if t >= 2:
                                pe.wait_ge(free, UNITS * c + t - 1)
                            s = slice(k * FF + f * P, k * FF + (f + 1) * P)
                            three(bank_[:, :], w_hi[:, e, s], w_lo[:, e, s], x2h[:, :], x2l[:, :]).then_inc(full, 1)
                    if t >= LAG:
                        u = t - LAG
                        e, f = divmod(u, FB)
                        pe.wait_ge(hl_done, UNITS * c + u + 1)
                        if f == 0:
                            pe.wait_ge(y_free, (EXPERTS + 1) * c + e)
                        s = slice(2 * FF + f * P, 2 * FF + (f + 1) * P)
                        three(y[:, :], w_hi[:, e, s], w_lo[:, e, s], hh[:, u % 2, :], hl[:, u % 2, :],
                              start=(f == 0), stop=(f == FB - 1)).then_inc(y_part, 1)
                pe.wait_ge(acc_done, EXPERTS * (c + 1))
                pe.wait_ge(y_free, (EXPERTS + 1) * c + EXPERTS)
                for b in range(CB):
                    last = turn(y[:, b * P:(b + 1) * P], acc[:, b * P:(b + 1) * P], P)
                last.then_inc(f_full, 1)

            with pe.Fori(0, CHUNKS) as c:
                attn(c)
                route(c)
                pe.wait_ge(w_lo_done, EXPERTS)
                ffn(c)


def kernel(**inputs):
    import numpy as np
    import concourse.bacc as bacc
    from concourse.bass_utils import run_bass_kernel_spmd

    def blocks(a):
        return a.reshape(EXPERTS, FB, P).transpose(2, 0, 1).reshape(P, UNITS)

    sel = np.zeros((P, EXPERTS), np.float32)
    for e in range(EXPERTS):
        sel[e, e] = 1
        sel[e + EXPERTS, e] = 1
    consts = np.concatenate([
        np.eye(P, dtype=np.float32),
        (np.arange(P)[:, None] // HD % HG == np.arange(HG)[None, :]).astype(np.float32),
        np.tile(np.arange(EXPERTS, dtype=np.float32), (P, 1)),
        (np.arange(P)[:, None] < 2 * EXPERTS).astype(np.float32),
        (np.arange(P)[:, None] >= 2 * EXPERTS).astype(np.float32),
        sel], axis=1)
    laid = {n: np.ascontiguousarray(a) for n, a in inputs.items()}
    laid["L0_ffn_b1"] = np.ascontiguousarray(blocks(laid["L0_ffn_b1"]))
    laid["L0_ffn_b3"] = np.ascontiguousarray(blocks(laid["L0_ffn_b3"]))
    laid["consts"] = consts
    names = ['x', 'ctx_1024', 'g_xattn', 'g_ffn', 'L0_xattn_Wq', 'L0_xattn_Wkv', 'L0_xattn_Wproj',
             'L0_xattn_q_gamma', 'L0_xattn_k_gamma', 'L0_ffn_Wg', 'L0_ffn_bg', 'L0_ffn_W1', 'L0_ffn_b1',
             'L0_ffn_W3', 'L0_ffn_b3', 'L0_ffn_W2', 'L0_ffn_b2', 'consts']
    nc = bacc.Bacc("TRN2", target_bir_lowering=False, num_devices=1)
    f32 = mybir.dt.float32
    arrays = {f"in_{n}": laid[n] for n in names}
    args = [nc.dram_tensor(f"in_{n}", laid[n].shape, f32, kind="ExternalInput").ap() for n in names]
    out = nc.dram_tensor("out_x", (NBATCH, P, D), f32, kind="ExternalOutput").ap()
    build(nc, *args, out)
    r = run_bass_kernel_spmd(nc, [arrays], core_ids=[0])
    return r.results[0]["out_x"]
```

```python
import concourse.bass as bass
from concourse import mybir
from concourse.alu_op_type import AluOpType as ALU
from contextlib import ExitStack

P = 128
NBATCH = 16
D = 128
HEADS = 16
HD = D // HEADS
KEYS = 77
FF = 512
EXPERTS = 8
CB = 4
CHUNKS = NBATCH // CB
CT = CB * P
FB = FF // P
UNITS = EXPERTS * FB
HG = 4
GROUPS = HEADS // HG
SLOT = 32
VW = HD + 1
VG = 8
VS = VG * VW
KVW = 2 * D
LN_EPS, RMS_EPS, TOP_EPS = 1e-5, 1e-6, 1e-6
MAGIC = 0x5F3759DF

LAG = 3
HB = LAG + 1
PB = 3

SCORES = (11.5, 14.5, 17.5, 20.5)
AT = {
    "cT": dict(pe=0.5, act=0.5, dve=0.6), "kv0": dict(pe=1.2, act=1.2), "kv1": dict(pe=2.0, act=2.0, dve=3.1),
    "ln0": dict(dve=0.5), "ln1": dict(dve=1.0), "ln2": dict(dve=1.5),
    "xT": dict(pe=2.8, act=3.0, dve=3.0), "q": dict(pe=4.0, act=4.0, dve=4.0),
    "rs0": dict(dve=4.6), "rs1": dict(dve=5.0), "kn": dict(dve=5.6), "qn": dict(dve=6.0),
    "qT": dict(pe=6.6, act=6.9), "kT": dict(pe=7.0, act=7.0),
    "oTT": dict(pe=24.2, act=24.2, dve=24.2), "proj": dict(pe=25.0, dve=25.0),
    "nrm": dict(dve=26.0), "ln3": dict(dve=27.0),
    "x2T": dict(pe=28.2, act=28.2, dve=28.2), "gate": dict(pe=29.0, act=29.7, dve=29.0),
    "top": dict(dve=30.2), "comb": dict(dve=30.6), "wT": dict(pe=31.8, act=31.8),
}
for _b in range(CB):
    _u = SCORES[_b]
    AT[f"klo{_b}"] = dict(dve=6.6 + 0.1 * _b)
    AT[f"kS{_b}"] = dict(pe=7.6 + 0.6 * _b, act=7.7 + 0.6 * _b)
    AT[f"qlo{_b}"] = dict(dve=_u - 1.7)
    AT[f"mA{_b}"] = dict(pe=_u - 1.3, dve=_u - 1.2)
    AT[f"mB{_b}"] = dict(pe=_u - 0.8, dve=_u - 0.8)
    AT[f"qS{_b}"] = dict(pe=_u - 0.5, act=_u - 0.5)
    AT[f"sA{_b}"] = dict(pe=_u, act=_u)
    AT[f"sB{_b}"] = dict(pe=_u + 0.9, act=_u + 0.1)
    AT[f"pv{_b}"] = dict(pe=_u + 2.0, act=_u + 2.1)
    AT[f"oT{_b}"] = dict(pe=_u + 3.1, dve=_u + 3.1)
    AT[f"kd{_b}"] = dict(pool=6.6 + 0.6 * _b)
    AT[f"kb{_b}"] = dict(pool=(9.3, 12.0, 15.0, 18.0)[_b])
    AT[f"va{_b}"] = dict(pool=_u + 0.2)
    AT[f"qd{_b}"] = dict(pool=_u - 1.6)
W_AT = (1.6, 5.6, 10.0, 12.6, 15.6, 18.6, 22.0, 26.6)
SIDE = {f"w{_e}": dict(pe=_t, act=_t) for _e, _t in enumerate(W_AT)}
SIDE["b2"] = dict(pe=2.6, act=2.6)
ALL_MIX = ["cT", "kv0", "kv1", "xT", "q", "qT", "kT", "oTT", "proj", "x2T", "gate", "wT"] + \
    [f"{n}{b}" for n in ("kS", "qS", "pv", "oT") for b in range(CB)]


def steps_of(engine):
    return sorted((t[engine], n) for n, t in AT.items() if engine in t)


def due(ph, engine, slot, late):
    first = slot + 0.5 * late
    table = {**(AT if ph.attn is not None else {}), **(SIDE if ph.ffn is not None else {})}
    return [n for t, n in sorted((t[engine], n) for n, t in table.items() if engine in t)
            if first <= t + 1e-9 < first + 0.5]


UNIT_GROUPS = {"mA": range(0, 2), "mB": range(2, 4), "sA": range(0, 2), "sB": range(2, 4)}

ALONE = [n for _, n in steps_of("pe") if n in ALL_MIX]
BOTH = [n for _, n in sorted((t["pe"], n) for n, t in {**AT, **SIDE}.items() if n in ALL_MIX or n in SIDE)]
LAST = [n for _, n in sorted((t["pe"], n) for n, t in SIDE.items())]
SCORE = {}
for _, _n in steps_of("pe"):
    for _g in UNIT_GROUPS.get(_n[:-1], ()):
        SCORE[("max" if _n[0] == "m" else "sc", int(_n[-1]), _g)] = len(SCORE)
NSCORE = len(SCORE) // 2
HIGH_AT = ["cT", "kv0", "kv1", "xT", "q", "kT", "kS1", "kS3"]
NLINK = 67


class Phase:

    def __init__(self, attn, ffn, base, order):
        self.attn, self.ffn, self.base, self.order = attn, ffn, base, order


def first_phase():
    return Phase(0, None, 0, ALONE)


def middle_phase(i):
    return Phase(i + 1, i, i * len(BOTH) + len(ALONE), BOTH)


def last_phase():
    return Phase(None, CHUNKS - 1, len(ALONE) + (CHUNKS - 1) * len(BOTH), LAST)


def build(nc, x, ctx_in, gx, gf, Wq, Wkv, Wproj, qg, kg, Wg, bg, W1, b1, W3, b3, W2, b2, consts, out):
    f32, f32r = mybir.dt.float32, mybir.dt.float32r
    i32, u32 = mybir.dt.int32, mybir.dt.uint32
    ACT, AX = mybir.ActivationFunctionType, mybir.AxisListType

    with ExitStack() as stack:
        def sb(name, shape, dt=f32):
            return stack.enter_context(nc.sbuf_tensor(name, shape, dt))

        def sem(name):
            return stack.enter_context(nc.semaphore(name))

        NCONST = consts.shape[1]
        cst = sb("cst", [P, NCONST])
        ident = cst[:, 0:P]
        hmask = cst[:, P:P + HG]
        iota = cst[:, P + HG:P + HG + EXPERTS]
        is_hi = cst[0:3 * EXPERTS, P + HG + EXPERTS:P + HG + EXPERTS + 1]
        is_lo = cst[0:3 * EXPERTS, P + HG + EXPERTS + 1:P + HG + EXPERTS + 2]
        sel_raw = cst[0:SLOT, P + HG + EXPERTS + 2:NCONST]
        sel = sb("sel", [SLOT, EXPERTS], f32r)
        acc = sb("acc", [P, CT])
        wq_raw, wp_raw, wkv_raw = acc[:, 0:D], acc[:, D:2 * D], acc[:, 2 * D:2 * D + KVW]
        wg_raw = sb("wg_raw", [D, EXPERTS])
        wq = sb("wq", [D, 2, D], f32r)
        wp = sb("wp", [D, 2, D], f32r)
        wkv = sb("wkv", [D, 2, KVW], f32r)
        wg = sb("wg", [D, 2, EXPERTS], f32r)
        EW = 3 * FF
        w_hi = sb("w_hi", [P, EXPERTS, EW], f32r)
        w_lo = sb("w_lo", [P, EXPERTS, EW], f32r)
        b1_sb, b3_sb = sb("b1_sb", [P, UNITS]), sb("b3_sb", [P, UNITS])
        bg_sb = sb("bg_sb", [P, EXPERTS])
        WR = 3 * EXPERTS
        b2_raw, b2_d = sb("b2_raw", [WR, D]), sb("b2_d", [WR, D])
        b2_hi, b2_s = sb("b2_hi", [WR, D], f32r), sb("b2_s", [WR, D], f32r)
        gates = sb("gates", [P, 2])
        gk = sb("gk", [KEYS, HD])
        gq = sb("gq", [KEYS, HD])

        xc = sb("xc", [P, CB, D])
        cc = sb("cc", [KEYS, CB, D])
        x1 = sb("x1", [P, 2 * CT])
        pad, one = sb("pad", [P, 1]), sb("one", [P, 1])
        stats = sb("stats", [P, CB, 6])
        mv = sb("mv", [P, CB, 2])
        xn = sb("xn", [P, CB, D])
        xh, xl = sb("xh", [D, CT], f32r), sb("xl", [D, CT], f32r)
        qr, sq = sb("qr", [P, CT]), xn[:, :, :].rearrange("p b d -> p (b d)")
        on = sb("on", [P, CB, D])
        kvr, ksq = sb("kvr", [KEYS, CB, KVW]), on[0:KEYS, :, :]
        NR = CB * HEADS
        ss = sb("ss", [P, 2 * NR])
        nt1, nt2, rinv = sb("nt1", [P, 2 * NR]), sb("nt2", [P, 2 * NR]), sb("rinv", [P, 2 * NR])
        qn, qhi = sb("qn", [P, CT]), sq.bitcast(f32r)
        kn, khi = sb("kn", [KEYS, CT]), on[0:KEYS, :, :].rearrange("p b d -> p (b d)").bitcast(f32r)
        q_st = sb("q_st", [P, CB, HEADS, SLOT])
        k_st = q_st[0:KEYS]
        qTh = sb("qTh", [D, CT], f32r)
        kT = qr[:, 0:CB * KEYS]
        k_bd = sb("k_bd", [D, CB, HG, KEYS], f32r)
        ksT = sb("ksT", [P, CB, GROUPS, KEYS], f32r)
        ch, cl = (ksT[:, b, :, :].rearrange("p i t -> p (i t)") for b in range(2))
        qsT = sb("qsT", [P, 2, GROUPS, P], f32r)
        probs = sb("probs", [KEYS, HG, GROUPS, P])
        va = sb("va", [KEYS, 1, 2, VG * (VS + VW)])
        oa = sb("oa", [VS, 2 * P])
        rden = sb("rden", [P, HEADS])
        oh, ol = xh, xl
        x2h, x2l = sb("x2h", [D, CT], f32r), sb("x2l", [D, CT], f32r)
        lg, ex, pr = sb("lg", [P, CB, EXPERTS]), sb("ex", [P, CB, EXPERTS]), sb("pr", [P, CB, EXPERTS])
        r4, s4 = sb("r4", [P, CB]), sb("s4", [P, CB])
        top = sb("top", [P, CB, 8])
        topi = sb("topi", [P, CB, 8], u32)
        topf = sb("topf", [P, CB, 8])
        e1, e2 = sb("e1", [P, CB, EXPERTS]), sb("e2", [P, CB, EXPERTS])
        chi = sb("chi", [P, CB, EXPERTS], f32r)
        c_st = sb("c_st", [P, CB, SLOT])
        cT = sb("cT", [SLOT, CT], f32r)
        cbc = sb("cbc", [P, 2, CT])
        arena = sb("arena", [P, 2 * EW])
        w_raw = arena[:, :].rearrange("p (k w) -> p k w", k=2)
        hf = arena[:, 0:HB * CT].rearrange("p (k t) -> p k t", k=HB)
        yt = arena[:, HB * CT:(HB + 2) * CT].rearrange("p (k t) -> p k t", k=2)
        outb = yt[:, 0, :]
        hh, hl = sb("hh", [P, PB, CT], f32r), sb("hl", [P, PB, CT], f32r)

        def bank(name):
            return stack.enter_context(nc.psum_tensor(name, [P, 512], f32))

        up, gt = [bank("up0"), bank("up1")], [bank("gt0"), bank("gt1")]
        y = bank("y")
        score = [bank("score0"), bank("score1")]
        mix = bank("mix")

        cst_in, small_in, bias_in = sem("cst_in"), sem("small_in"), sem("bias_in")
        w_in = [sem("w_in0"), sem("w_in1")]
        outb_free = sem("outb_free")
        x_in, c_in, out_done = sem("x_in"), sem("c_in"), sem("out_done")
        small_hi, small_lo = sem("small_hi"), sem("small_lo")
        w_hi_done, w_lo_done = sem("w_hi_done"), sem("w_lo_done")
        init_done, tanh_done, b2_hi_done = sem("init_done"), sem("tanh_done"), sem("b2_hi_done")
        gk_done = sem("gk_done")
        link_s = sem("link_s")
        mix_full, mix_free = sem("mix_full"), sem("mix_free")
        score_full = sem("score_full")
        score_free = [sem("score_free0"), sem("score_free1")]
        xn_done, xh_done, ch_done = sem("xn_done"), sem("xh_done"), sem("ch_done")
        qsq_done, ksq_done = sem("qsq_done"), sem("ksq_done")
        qn_done, kn_done, qhi_done, khi_done = sem("qn_done"), sem("kn_done"), sem("qhi_done"), sem("khi_done")
        qdup_done, kdup_done, klo_done = sem("qdup_done"), sem("kdup_done"), sem("klo_done")
        kbd_done, va_done = sem("kbd_done"), sem("va_done")
        pv_half = sem("pv_half")
        shift_done, on_done, oh_done, x1_done = sem("shift_done"), sem("on_done"), sem("oh_done"), sem("x1_done")
        xn2_done, x2h_done = sem("xn2_done"), sem("x2h_done")
        lg_done, ex_done, cst_done = sem("lg_done"), sem("ex_done"), sem("cst_done")
        up_full, gt_full = sem("up_full"), sem("gt_full")
        sil_done, h_done, hh_done, hl_done = sem("sil_done"), sem("h_done"), sem("hh_done"), sem("hl_done")
        y_part, y_free, acc_done, f_full = sem("y_part"), sem("y_free"), sem("acc_done"), sem("f_full")

        block = stack.enter_context(nc.Block())

        def mix_at(ph, name):
            return ph.base + (ph.order.index(name) + 1)

        def mix_before(ph, name):
            return ph.base + ph.order.index(name)

        def score_at(c, kind, b, g):
            return len(SCORE) * c + SCORE[(kind, b, g)] + 1

        def score_bank(kind, b, g):
            return SCORE[(kind, b, g)] % 2

        def score_before(c, kind, b, g):
            return NSCORE * c + SCORE[(kind, b, g)] // 2

        def y_reads(c, n):
            return (EXPERTS + 1) * c + n + 1

        def units(c, n):
            return UNITS * c + n

        def x1_chunk(c):
            return x1[:, bass.ds((c % 2) * CT, CT)]

        @block.sync
        def _(sp):
            sp.dma_start(cst[:, :], consts).then_inc(cst_in, 16)
            sp.dma_start(wq_raw[:, :], Wq).then_inc(small_in, 16)
            sp.dma_start(wkv_raw[:, :], Wkv).then_inc(small_in, 16)
            sp.dma_start(wp_raw[:, :], Wproj).then_inc(small_in, 16)
            sp.dma_start(wg_raw[:, :], Wg).then_inc(small_in, 16)
            sp.dma_start(gates[:, 0:1], gx.partition_broadcast(P)).then_inc(bias_in, 16)
            sp.dma_start(gates[:, 1:2], gf.partition_broadcast(P)).then_inc(bias_in, 16)
            sp.dma_start(gq[:, :], qg.partition_broadcast(KEYS)).then_inc(bias_in, 16)
            sp.dma_start(gk[:, :], kg.partition_broadcast(KEYS)).then_inc(bias_in, 16)
            sp.dma_start(bg_sb[:, :], bg.partition_broadcast(P)).then_inc(bias_in, 16)
            sp.dma_start(b1_sb[:, :], b1).then_inc(bias_in, 16)
            sp.dma_start(b3_sb[:, :], b3).then_inc(bias_in, 16)
            for k in range(3):
                sp.dma_start(b2_raw[EXPERTS * k:EXPERTS * (k + 1), :], b2).then_inc(bias_in, 16)
            def load_weights():
                for e in range(EXPERTS):
                    if e >= 2:
                        sp.wait_ge(w_hi_done, e - 1)
                        sp.wait_ge(w_lo_done, e - 1)
                    dst = w_raw[:, e % 2, :]
                    sp.dma_start(dst[:, 0:FF], W1[e, :, :]).then_inc(w_in[e % 2], 16)
                    sp.dma_start(dst[:, FF:2 * FF], W3[e, :, :]).then_inc(w_in[e % 2], 16)
                    sp.dma_start(dst[:, 2 * FF:EW].rearrange("p (f d) -> p f d", f=FB),
                                 W2[e, :, :].rearrange("(f p) d -> p f d", p=P)).then_inc(w_in[e % 2], 16)

            def load(c):
                sp.dma_start(xc[:, :, :], x[bass.ds(c * CB, CB), :, :].rearrange("b p d -> p b d")).then_inc(x_in, 16)
                sp.dma_start(cc[:, :, :], ctx_in[bass.ds(c * CB, CB), :, :].rearrange("b p d -> p b d")).then_inc(c_in, 16)

            def store(c):
                sp.wait_ge(y_free, y_reads(c, EXPERTS + 1))
                sp.dma_start(out[bass.ds(c * CB, CB), :, :].rearrange("b p d -> p b d"),
                             outb.rearrange("p (b d) -> p b d", b=CB)).then_inc(out_done, 16)
                sp.wait_ge(out_done, 16 * c + 16)
                sp.sem_inc(outb_free, 1)

            load(0)
            load_weights()
            with sp.Fori(0, CHUNKS - 1) as i:
                sp.wait_ge(x1_done, i + 1)
                load(i + 1)
                store(i)
            store(CHUNKS - 1)

        @block.gpsimd
        def _(pool):
            def same(dst, src):
                ones = one[0:src.shape[0], :]
                while len(ones.shape) < len(src.shape):
                    ones = ones.unsqueeze(1)
                return nc.gpsimd.tensor_tensor(dst, src, ones.to_broadcast(list(src.shape)), ALU.mult)

            def split(e):
                pool.wait_ge(w_hi_done, e + 1)
                nc.gpsimd.tensor_tensor(w_lo[:, e, :], w_raw[:, e % 2, :], w_hi[:, e, :].bitcast(f32),
                                        ALU.subtract).then_inc(w_lo_done, 1)

            def heads(ap):
                return ap.rearrange("p (h d) -> p h d", d=HD)

            def attn(ph, n):
                c, b = ph.attn, int(n[-1])
                if n[:2] == "kd":
                    pool.wait_ge(khi_done, c + 1)
                    src = heads(khi[:, b * D:(b + 1) * D].bitcast(f32))
                    same(k_st[:, b, :, 0:HD], src).then_inc(kdup_done, 1)
                    same(k_st[:, b, :, HD:2 * HD], src).then_inc(kdup_done, 1)
                elif n[:2] == "kb":
                    pool.wait_ge(mix_free, mix_at(ph, "kT"))
                    nc.gpsimd.tensor_tensor(
                        k_bd[:, b, :, :], kT[:, b * KEYS:(b + 1) * KEYS].unsqueeze(1).to_broadcast([D, HG, KEYS]),
                        hmask.unsqueeze(2).to_broadcast([D, HG, KEYS]), ALU.mult).then_inc(kbd_done, 1)
                elif n[:2] == "va":
                    if b == 0:
                        pool.wait_ge(mix_free, mix_at(ph, "kv1"))
                    else:
                        pool.wait_ge(mix_full, mix_at(ph, f"pv{b - 1}"))
                    for g in range(2):
                        src = kvr[:, b, D:2 * D].rearrange("p (i g j d) -> p i g j d", i=GROUPS, g=2, d=HD)[:, :, g]
                        dst = va[:, 0, g, :].rearrange("p (i j s) -> p i j s", i=GROUPS, j=2)[:, :, :, 0:HD]
                        same(dst, src).then_inc(va_done, 1)
                elif n[:2] == "qd":
                    pool.wait_ge(mix_full, mix_at(ph, "kS3"))
                    pool.wait_ge(qhi_done, c + 1)
                    src = heads(qhi[:, b * D:(b + 1) * D].bitcast(f32))
                    same(q_st[:, b, :, 0:HD], src).then_inc(qdup_done, 1)
                    same(q_st[:, b, :, 2 * HD:3 * HD], src).then_inc(qdup_done, 1)

            def low(c, t):
                pool.wait_ge(hh_done, units(c, t + 1))
                nc.gpsimd.tensor_tensor(hl[:, t % PB, :], hf[:, t % HB, :], hh[:, t % PB, :].bitcast(f32),
                                        ALU.subtract).then_inc(hl_done, 1)

            def add_y(ph, e):
                c = ph.ffn
                pool.wait_ge(y_free, y_reads(c, e + 1))
                if e == 0:
                    pool.wait_ge(mix_free, mix_at(ph, "b2"))
                else:
                    pool.wait_ge(acc_done, EXPERTS * c + e)
                nc.gpsimd.tensor_tensor(acc[:, :], acc[:, :], yt[:, e % 2, :], ALU.add).then_inc(acc_done, 1)

            def ffn(ph, s):
                for late in (0, 1):
                    if late:
                        t = s + LAG - 1
                        if t < UNITS:
                            low(ph.ffn, t)
                        elif ph.attn is not None:
                            low(ph.attn, t - UNITS)
                        if s % FB == 0 and s > 0:
                            add_y(ph, s // FB - 1)
                    for n in due(ph, "pool", s, late):
                        attn(ph, n)

            pool.wait_ge(init_done, 4)
            ph = first_phase()
            for e in range(3):
                split(e)
            for k, (_, n) in enumerate(steps_of("pool")):
                attn(ph, n)
                if k < 5:
                    split(3 + k)
            for t in range(LAG - 1):
                low(0, t)
            with pool.Fori(0, CHUNKS - 1) as i:
                ph = middle_phase(i)
                for s in range(UNITS):
                    ffn(ph, s)
                add_y(ph, EXPERTS - 1)
            ph = last_phase()
            for s in range(UNITS):
                ffn(ph, s)
            add_y(ph, EXPERTS - 1)

        @block.scalar
        def _(act):
            act.wait_ge(small_in, 64)
            nc.scalar.copy(wq[:, 0, :], wq_raw[:, :]).then_inc(small_hi, 1)
            nc.scalar.copy(wkv[:, 0, :], wkv_raw[:, :]).then_inc(small_hi, 1)
            nc.scalar.copy(wp[:, 0, :], wp_raw[:, :]).then_inc(small_hi, 1)
            nc.scalar.copy(wg[:, 0, :], wg_raw[:, :]).then_inc(small_hi, 1)
            act.wait_ge(cst_in, 16)
            nc.scalar.copy(sel[:, :], sel_raw).then_inc(small_hi, 1)
            act.wait_ge(bias_in, 160)
            nc.scalar.activation(gates[:, :], gates[:, :], ACT.Tanh).then_inc(tanh_done, 1)
            nc.scalar.copy(b2_hi[:, :], b2_raw[:, :]).then_inc(b2_hi_done, 1)

            def split(e):
                act.wait_ge(w_in[e % 2], 48 * (e // 2 + 1))
                nc.scalar.copy(w_hi[:, e, :], w_raw[:, e % 2, :]).then_inc(w_hi_done, 1)

            def attn(ph, n):
                c = ph.attn
                if n[:2] in ("sA", "sB"):
                    b = int(n[2:])
                    for j in UNIT_GROUPS[n[:2]]:
                        k = score_bank("sc", b, j)
                        act.wait_ge(score_full, score_at(c, "sc", b, j))
                        if b >= 1 and j == 0:
                            act.wait_ge(pv_half, CB * c + b)
                        if b >= 1 and j == 2:
                            act.wait_ge(mix_full, mix_at(ph, f"pv{b - 1}"))
                        nc.scalar.activation(probs[:, j, :, :].rearrange("p i t -> p (i t)"),
                                             score[k][0:KEYS, :], ACT.Exp).then_inc(score_free[k], 1)
                    return
                if n == "gate":
                    act.wait_ge(lg_done, c + 1)
                    nc.scalar.activation(ex[:, :, :], lg[:, :, :], ACT.Exp).then_inc(ex_done, 1)
                    return
                act.wait_ge(mix_full, mix_at(ph, n))
                if n == "xT":
                    nc.scalar.copy(xh[:, :], mix[:, :]).then_inc(xh_done, 1)
                elif n == "q":
                    nc.scalar.activation(sq[:, :], mix[:, :], ACT.Square).then_inc(qsq_done, 1)
                    nc.scalar.copy(qr[:, :], mix[:, :]).then_inc(mix_free, 1)
                elif n == "cT":
                    nc.scalar.copy(ch[:, :], mix[:, 0:CB * KEYS]).then_inc(ch_done, 1)
                elif n[:2] == "kv":
                    a = 2 * int(n[2:])
                    src = mix[0:KEYS, :].rearrange("p (b w) -> p b w", b=2)
                    nc.scalar.activation(ksq[:, a:a + 2, :], src[:, :, 0:D], ACT.Square).then_inc(ksq_done, 1)
                    nc.scalar.copy(kvr[:, a:a + 2, :], src).then_inc(mix_free, 1)
                elif n == "qT":
                    nc.scalar.copy(qTh[:, :], mix[:, :]).then_inc(mix_free, 1)
                elif n == "kT":
                    nc.scalar.copy(kT[:, :], mix[:, 0:CB * KEYS]).then_inc(mix_free, 1)
                elif n[:2] == "kS":
                    b = int(n[2:])
                    nc.scalar.copy(ksT[:, b, :, :].rearrange("p i t -> p (i t)"),
                                   mix[:, 0:GROUPS * KEYS]).then_inc(mix_free, 1)
                elif n[:2] == "qS":
                    b = int(n[2:])
                    nc.scalar.copy(qsT[:, b % 2, :, :].rearrange("p i t -> p (i t)"),
                                   mix[:, :]).then_inc(mix_free, 1)
                elif n[:2] == "pv":
                    nc.scalar.copy(oa[:, :], mix[0:VS, 0:2 * P]).then_inc(mix_free, 1)
                elif n == "oTT":
                    nc.scalar.copy(oh[:, :], mix[:, :]).then_inc(oh_done, 1)

                elif n == "x2T":
                    act.wait_ge(gt_full, UNITS * c)
                    nc.scalar.copy(x2h[:, :], mix[:, :]).then_inc(x2h_done, 1)
                elif n == "wT":
                    nc.scalar.copy(cT[:, :], mix[0:SLOT, :]).then_inc(mix_free, 1)

            def spread(ph, n):
                act.wait_ge(mix_full, mix_at(ph, n))
                if n == "b2":
                    act.wait_ge(y_free, y_reads(ph.ffn, 0))
                    nc.scalar.copy(acc[:, :], mix[:, :]).then_inc(mix_free, 1)
                    return
                e = int(n[1:])
                if e >= 2:
                    act.wait_ge(y_free, y_reads(ph.ffn, e - 1))
                nc.scalar.copy(cbc[:, e % 2, :], mix[:, :]).then_inc(mix_free, 1)

            def silu(c, t, fresh=False):
                act.wait_ge(up_full, units(c, t + 1))
                if not fresh:
                    act.wait_ge(hl_done, units(c, 1 if t == LAG else t + 1 - HB))
                nc.scalar.activation(hf[:, t % HB, :], up[t % 2][:, :], ACT.Silu,
                                     bias=b1_sb[:, t:t + 1]).then_inc(sil_done, 1)

            def high(c, t, fresh=False):
                act.wait_ge(h_done, units(c, t + 1))
                if t >= PB:
                    act.wait_ge(y_part, units(c, t + 1 - PB))
                elif t < 2 and not fresh:
                    act.wait_ge(y_part, units(c, t - 1))
                nc.scalar.copy(hh[:, t % PB, :], hf[:, t % HB, :]).then_inc(hh_done, 1)

            def ffn(ph, s):
                c, nxt = ph.ffn, ph.attn
                for late in (0, 1):
                    for part, t in ((high, s + LAG - 1),) if late else ((silu, s + LAG),):
                        if t < UNITS:
                            part(c, t)
                        elif nxt is not None:
                            part(nxt, t - UNITS)
                    for n in due(ph, "act", s, late):
                        (spread if n in SIDE else attn)(ph, n)

            ph = first_phase()
            for _, n in steps_of("act"):
                attn(ph, n)
                if n in HIGH_AT:
                    split(HIGH_AT.index(n))
            act.wait_ge(w_lo_done, EXPERTS)
            for t in range(LAG):
                silu(0, t, fresh=True)
                if t >= 1:
                    high(0, t - 1, fresh=True)
            with act.Fori(0, CHUNKS - 1) as i:
                ph = middle_phase(i)
                for s in range(UNITS):
                    ffn(ph, s)
            ph = last_phase()
            for s in range(UNITS):
                ffn(ph, s)

        @block.vector
        def _(dve):
            ve = nc.vector
            ve.memset(q_st[:, :, :, :], 0.0).then_inc(init_done, 1)
            ve.memset(c_st[:, :, :], 0.0).then_inc(init_done, 1)
            ve.memset(va[:, :, :, :], 0.0).then_inc(init_done, 1)
            dve.wait_ge(init_done, 3)
            for g in range(2):
                ve.memset(va[:, 0, g, :].rearrange("p (h s) -> p h s", h=VG)[:, :, HD:HD + 1], 1.0)
            ve.memset(one[:, :], 1.0)
            ve.memset(pad[:, :], 0.0).then_inc(outb_free, 1)
            ve.memset(rden[:, :], 0.0).then_inc(y_free, 1)
            ve.memset(ss[:, :], 1.0).then_inc(init_done, 1)
            dve.wait_ge(bias_in, 160)
            dve.wait_ge(cst_in, 16)
            dve.wait_ge(init_done, 4)
            ve.scalar_tensor_tensor(out=gk[:, :], in0=gk[:, :], scalar=float(HD) ** -0.5, in1=gq[:, :],
                                    op0=ALU.mult, op1=ALU.mult).then_inc(gk_done, 1)
            dve.wait_ge(b2_hi_done, 1)
            ve.tensor_tensor(b2_d[:, :], b2_raw[:, :], b2_hi[:, :].bitcast(f32), ALU.subtract).then_inc(gk_done, 1)
            dve.wait_ge(gk_done, 2)
            ve.tensor_scalar(b2_raw[:, :], b2_hi[:, :].bitcast(f32), is_hi, None, ALU.mult).then_inc(gk_done, 1)
            dve.wait_ge(gk_done, 3)
            ve.scalar_tensor_tensor(out=b2_s[:, :], in0=b2_d[:, :], scalar=is_lo, in1=b2_raw[:, :],
                                    op0=ALU.mult, op1=ALU.add).then_inc(gk_done, 1)
            for k, (raw, hi, lo) in enumerate([(wq_raw[:, :], wq[:, 0, :], wq[:, 1, :]),
                                               (wkv_raw[:, :], wkv[:, 0, :], wkv[:, 1, :]),
                                               (wp_raw[:, :], wp[:, 0, :], wp[:, 1, :]),
                                               (wg_raw[:, :], wg[:, 0, :], wg[:, 1, :])]):
                dve.wait_ge(small_hi, k + 1)
                ve.tensor_tensor(lo, raw, hi.bitcast(f32), ALU.subtract).then_inc(small_lo, 1)

            links = [0]

            def link(c, ins):
                links[0] += 1
                ins.then_inc(link_s, 1)
                dve.wait_ge(link_s, NLINK * c + links[0])

            def hold():
                return ve.memset(pad[:, :], 0.0)

            def guess(c, v, dst, t1):
                link(c, ve.tensor_scalar(t1.bitcast(i32), v.bitcast(i32), 1, None, ALU.logical_shift_right))
                link(c, ve.tensor_scalar(dst.bitcast(i32), t1.bitcast(i32), -1.0, float(MAGIC), ALU.mult, ALU.add))
                link(c, ve.tensor_scalar(v, v, -0.5, None, ALU.mult))

            def newton(c, v, dst, t1, t2, steps=3):
                for _ in range(steps):
                    link(c, ve.tensor_tensor(t1, dst, dst, ALU.mult))
                    link(c, ve.tensor_tensor(t2, t1, v, ALU.mult))
                    link(c, ve.scalar_tensor_tensor(out=dst, in0=t2, scalar=1.5, in1=dst,
                                                    op0=ALU.add, op1=ALU.mult))

            NORM = (s4[:, :], r4[:, :], nt1[:, 0:CB], nt2[:, 0:CB])

            def moments(c, src):
                for b in range(CB):
                    ins = ve.bn_stats(stats[:, b, :], src[:, b, :])
                link(c, ins)
                hold()
                for b in range(CB):
                    ins = ve.bn_aggr(mv[:, b, :], stats[:, b, :])
                link(c, ins)
                link(c, ve.tensor_scalar(s4[:, :], mv[:, :, 1], LN_EPS, None, ALU.add))
                guess(c, *NORM[0:3])

            def normed(src):
                for b in range(CB):
                    ins = ve.tensor_scalar(xn[:, b, :], src[:, b, :], mv[:, b, 0:1], r4[:, b:b + 1],
                                           ALU.subtract, ALU.mult)
                return ins

            def heads(ap):
                return ap.rearrange("p (h d) -> p h d", d=HD)

            ROOTS = (ss[:, :], rinv[:, :], nt1[:, :], nt2[:, :])

            def attn(ph, n):
                c = ph.attn
                if n == "ln0":
                    ve.memset(k_st[:, :, :, 3 * HD:3 * HD + 1], 1.0)
                    dve.wait_ge(x_in, 16 * c + 16)
                    hold()
                    moments(c, xc)
                elif n == "ln1":
                    newton(c, *NORM)
                elif n == "ln2":
                    normed(xc).then_inc(xn_done, 1)
                elif n == "xT":
                    dve.wait_ge(xh_done, c + 1)
                    ve.tensor_tensor(xl[:, :], mix[:, :], xh[:, :].bitcast(f32), ALU.subtract).then_inc(mix_free, 1)
                elif n == "q":
                    dve.wait_ge(qsq_done, c + 1)
                    link(c, ve.tensor_reduce(ss[:, 0:NR], heads(sq[:, :]), AX.X, ALU.add))
                    link(c, ve.tensor_scalar(ss[:, :], ss[:, :], 1.0 / HD, RMS_EPS, ALU.mult, ALU.add))
                elif n == "cT":
                    dve.wait_ge(ch_done, c + 1)
                    ve.tensor_tensor(cl[:, :], mix[:, 0:CB * KEYS], ch[:, :].bitcast(f32),
                                     ALU.subtract).then_inc(mix_free, 1)
                elif n == "kv1":
                    dve.wait_ge(ksq_done, 2 * c + 2)
                    link(c, ve.tensor_reduce(ss[0:KEYS, NR:2 * NR],
                                             heads(ksq[:, :, :].rearrange("p b d -> p (b d)")), AX.X, ALU.add))
                elif n == "rs0":
                    guess(c, *ROOTS[0:3])
                    newton(c, *ROOTS, steps=1)
                elif n == "rs1":
                    newton(c, *ROOTS, steps=2)
                elif n == "kn":
                    dve.wait_ge(mix_free, mix_at(ph, "q"))
                    rk = rinv[0:KEYS, NR:2 * NR]
                    for b in range(CB):
                        ins = ve.tensor_tensor(heads(kn[:, b * D:(b + 1) * D]), heads(kvr[:, b, 0:D]),
                                               rk[:, b * HEADS:(b + 1) * HEADS].unsqueeze(2)
                                               .to_broadcast([KEYS, HEADS, HD]), ALU.mult)
                    link(c, ins)
                    ve.tensor_tensor(heads(kn[:, :]), heads(kn[:, :]),
                                     gk[:, :].unsqueeze(1).to_broadcast([KEYS, NR, HD]), ALU.mult).then_inc(kn_done, 1)
                elif n == "qn":
                    ve.tensor_tensor(heads(qn[:, :]), heads(qr[:, :]),
                                     rinv[:, 0:NR].unsqueeze(2).to_broadcast([P, NR, HD]), ALU.mult).then_inc(qn_done, 1)
                    dve.wait_ge(kn_done, c + 1)
                    ve.tensor_copy(khi[:, :], kn[:, :]).then_inc(khi_done, 1)
                    dve.wait_ge(qn_done, c + 1)
                    ve.tensor_copy(qhi[:, :], qn[:, :]).then_inc(qhi_done, 1)
                elif n[:3] == "klo":
                    b = int(n[3:])
                    dve.wait_ge(khi_done, c + 1)
                    ve.tensor_tensor(k_st[:, b, :, 2 * HD:3 * HD], heads(kn[:, b * D:(b + 1) * D]),
                                     heads(khi[:, b * D:(b + 1) * D].bitcast(f32)),
                                     ALU.subtract).then_inc(klo_done, 1)
                elif n[:3] == "qlo":
                    b = int(n[3:])
                    dve.wait_ge(qhi_done, c + 1)
                    dve.wait_ge(mix_full, mix_at(ph, "kS3"))
                    ve.tensor_tensor(q_st[:, b, :, HD:2 * HD], heads(qn[:, b * D:(b + 1) * D]),
                                     heads(qhi[:, b * D:(b + 1) * D].bitcast(f32)), ALU.subtract)
                elif n[:2] in ("mA", "mB"):
                    b = int(n[2:])
                    for g in UNIT_GROUPS[n[:2]]:
                        k = score_bank("max", b, g)
                        dve.wait_ge(score_full, score_at(c, "max", b, g))
                        src = score[k][:, 0:HG * KEYS].rearrange("p (h t) -> p h t", h=HG)
                        ve.tensor_reduce(q_st[:, b, HG * g:HG * (g + 1), 3 * HD], src, AX.X, ALU.max,
                                         negate=True).then_inc(score_free[k], 1)
                elif n == "oTT":
                    dve.wait_ge(oh_done, c + 1)
                    ve.tensor_tensor(ol[:, :], mix[:, :], oh[:, :].bitcast(f32), ALU.subtract).then_inc(mix_free, 1)
                elif n[:2] == "oT":
                    b = int(n[2:])
                    dve.wait_ge(mix_full, mix_at(ph, n))
                    o = mix[:, 0:2 * VS].rearrange("p (h s) -> p h s", s=VW)
                    link(c, ve.reciprocal(rden[:, :], o[:, :, HD]))
                    for g in range(2):
                        ins = ve.tensor_tensor(
                            on[:, b, :].rearrange("p (i g j d) -> p i g j d", i=GROUPS, g=2, d=HD)[:, :, g],
                            o[:, g * VG:(g + 1) * VG, 0:HD].rearrange("p (i j) d -> p i j d", j=2),
                            rden[:, g * VG:(g + 1) * VG].rearrange("p (i j) -> p i j", j=2)
                            .unsqueeze(3).to_broadcast([P, GROUPS, 2, HD]), ALU.mult)
                    ins.then_inc(mix_free, 1)
                elif n == "proj":
                    dve.wait_ge(mix_full, mix_at(ph, "proj"))
                    dve.wait_ge(tanh_done, 1)
                    ve.scalar_tensor_tensor(out=x1_chunk(c), in0=mix[:, :], scalar=gates[:, 0:1],
                                            in1=xc[:, :, :].rearrange("p b d -> p (b d)"),
                                            op0=ALU.mult, op1=ALU.add).then_inc(mix_free, 1)
                    dve.wait_ge(mix_free, mix_at(ph, "proj"))
                    hold().then_inc(x1_done, 1)
                elif n == "nrm":
                    moments(c, x1_chunk(c).rearrange("p (b d) -> p b d", b=CB))
                elif n == "ln3":
                    newton(c, *NORM)
                    normed(x1_chunk(c).rearrange("p (b d) -> p b d", b=CB)).then_inc(xn2_done, 1)
                elif n in ("x2T", "gate", "top", "comb"):
                    route(ph, n)

            def route(ph, n):
                c = ph.attn
                if n == "x2T":
                    dve.wait_ge(x2h_done, c + 1)
                    ve.tensor_tensor(x2l[:, :], mix[:, :], x2h[:, :].bitcast(f32),
                                     ALU.subtract).then_inc(mix_free, 1)
                elif n == "gate":
                    logits(ph)
                elif n == "top":
                    top_two(ph)
                else:
                    combine(ph)

            def logits(ph):
                c = ph.attn
                dve.wait_ge(mix_full, mix_at(ph, "gate"))
                ve.tensor_tensor(lg[:, :, :], mix[:, 0:CB * EXPERTS].rearrange("p (b e) -> p b e", b=CB),
                                 bg_sb[:, :].unsqueeze(1).to_broadcast([P, CB, EXPERTS]),
                                 ALU.add).then_inc(mix_free, 1)
                dve.wait_ge(mix_free, mix_at(ph, "gate"))
                link(c, ve.tensor_reduce(r4[:, :], lg[:, :, :], AX.X, ALU.max))
                ve.tensor_tensor(lg[:, :, :], lg[:, :, :], r4[:, :].unsqueeze(2).to_broadcast([P, CB, EXPERTS]),
                                 ALU.subtract).then_inc(lg_done, 1)

            def top_two(ph):
                c = ph.attn
                dve.wait_ge(ex_done, c + 1)
                link(c, ve.tensor_reduce(s4[:, :], ex[:, :, :], AX.X, ALU.add))
                link(c, ve.reciprocal(r4[:, :], s4[:, :]))
                link(c, ve.tensor_tensor(pr[:, :, :], ex[:, :, :],
                                         r4[:, :].unsqueeze(2).to_broadcast([P, CB, EXPERTS]), ALU.mult))
                hold()
                for b in range(CB):
                    ins = ve.max(top[:, b, :], pr[:, b, :])
                link(c, ins)
                hold()
                for b in range(CB):
                    ins = ve.max_index(topi[:, b, :], top[:, b, :], pr[:, b, :])
                link(c, ins)
                link(c, ve.tensor_copy(topf[:, :, 0:2], topi[:, :, 0:2]))

            def combine(ph):
                c = ph.attn
                link(c, ve.tensor_tensor(s4[:, :], top[:, :, 0], top[:, :, 1], ALU.add))
                link(c, ve.tensor_scalar(s4[:, :], s4[:, :], TOP_EPS, None, ALU.add))
                link(c, ve.reciprocal(r4[:, :], s4[:, :]))
                link(c, ve.tensor_tensor(top[:, :, 0:2], top[:, :, 0:2],
                                         r4[:, :].unsqueeze(2).to_broadcast([P, CB, 2]), ALU.mult))
                io = iota.unsqueeze(1).to_broadcast([P, CB, EXPERTS])
                for k, e in enumerate((e1, e2)):
                    link(c, ve.tensor_tensor(e[:, :, :], io, topf[:, :, k:k + 1].to_broadcast([P, CB, EXPERTS]),
                                             ALU.is_equal))
                    link(c, ve.tensor_tensor(e[:, :, :], e[:, :, :],
                                             top[:, :, k:k + 1].to_broadcast([P, CB, EXPERTS]), ALU.mult))
                link(c, ve.tensor_tensor(e1[:, :, :], e1[:, :, :], e2[:, :, :], ALU.add))
                link(c, ve.tensor_copy(chi[:, :, :], e1[:, :, :]))
                ve.tensor_copy(c_st[:, :, 0:EXPERTS], chi[:, :, :].bitcast(f32))
                ve.tensor_copy(c_st[:, :, 2 * EXPERTS:3 * EXPERTS], chi[:, :, :].bitcast(f32))
                ve.tensor_tensor(c_st[:, :, EXPERTS:2 * EXPERTS], e1[:, :, :], chi[:, :, :].bitcast(f32),
                                 ALU.subtract).then_inc(cst_done, 1)

            def weigh_y(ph, e):
                c = ph.ffn
                dve.wait_ge(y_part, UNITS * c + FB * (e + 1))
                dve.wait_ge(mix_free, mix_at(ph, f"w{e}"))
                if e == 0:
                    dve.wait_ge(outb_free, c + 1)
                if e >= 2:
                    dve.wait_ge(acc_done, EXPERTS * c + e - 1)
                ve.tensor_tensor(yt[:, e % 2, :], y[:, :], cbc[:, e % 2, :], ALU.mult).then_inc(y_free, 1)

            def hidden(c, t):
                dve.wait_ge(gt_full, units(c, t + 1))
                dve.wait_ge(sil_done, units(c, t + 1))
                ve.scalar_tensor_tensor(out=hf[:, t % HB, :], in0=gt[t % 2][:, :], scalar=b3_sb[:, t:t + 1],
                                        in1=hf[:, t % HB, :], op0=ALU.add, op1=ALU.mult).then_inc(h_done, 1)

            def ffn(ph, s):
                if s + LAG < UNITS:
                    hidden(ph.ffn, s + LAG)
                elif ph.attn is not None:
                    hidden(ph.attn, s + LAG - UNITS)
                for late in (0, 1):
                    if late and s % FB == FB - 1 and s < UNITS - 1:
                        weigh_y(ph, s // FB)
                    for n in due(ph, "dve", s, late):
                        attn(ph, n)

            def finish(ph):
                c = ph.ffn
                weigh_y(ph, EXPERTS - 1)
                dve.wait_ge(f_full, c + 1)
                ve.scalar_tensor_tensor(out=outb, in0=y[:, :], scalar=gates[:, 1:2], in1=x1_chunk(c),
                                        op0=ALU.mult, op1=ALU.add).then_inc(y_free, 1)

            ph = first_phase()
            for _, n in steps_of("dve"):
                attn(ph, n)
            assert links[0] == NLINK, links[0]
            for t in range(LAG):
                hidden(0, t)
            with dve.Fori(0, CHUNKS - 1) as i:
                ph = middle_phase(i)
                links[0] = 0
                for s in range(UNITS):
                    ffn(ph, s)
                finish(ph)
            assert links[0] == NLINK, links[0]
            ph = last_phase()
            for s in range(UNITS):
                ffn(ph, s)
            finish(ph)

        @block.tensor
        def _(pe):
            pe.wait_ge(cst_in, 16)
            pe.wait_ge(small_hi, 5)
            pe.wait_ge(small_lo, 4)

            def three(dst, a_hi, a_lo, b_hi, b_lo, start=True, stop=True):
                nc.tensor.matmul(dst, a_hi, b_hi, start=start, stop=False)
                nc.tensor.matmul(dst, a_lo, b_hi, start=False, stop=False)
                return nc.tensor.matmul(dst, a_hi, b_lo, start=False, stop=stop)

            def turn(dst, src, n):
                return nc.tensor.transpose(dst, src, ident[0:n, 0:n])

            def attn(ph, n):
                c = ph.attn
                if n[:-1] in UNIT_GROUPS:
                    kind, b = "max" if n[0] == "m" else "sc", int(n[-1])
                    if kind == "max":
                        pe.wait_ge(kbd_done, CB * c + b + 1)
                    if n[:2] == "sA":
                        pe.wait_ge(mix_free, mix_at(ph, f"qS{b}"))
                    for g in UNIT_GROUPS[n[:-1]]:
                        k = score_bank(kind, b, g)
                        pe.wait_ge(score_free[k], score_before(c, kind, b, g))
                        r = slice(SLOT * g, SLOT * (g + 1))
                        if kind == "max":
                            last = nc.tensor.matmul(score[k][:, 0:HG * KEYS], qTh[r, b * P:(b + 1) * P],
                                                    k_bd[r, b, :, :].rearrange("p h t -> p (h t)"),
                                                    start=True, stop=True)
                        else:
                            for i in range(GROUPS):
                                last = nc.tensor.matmul(score[k][0:KEYS, i * P:(i + 1) * P],
                                                        ksT[r, b, i, :], qsT[r, b % 2, i, :],
                                                        start=True, stop=True)
                        last.then_inc(score_full, 1)
                    return
                if n == "xT":
                    pe.wait_ge(xn_done, c + 1)
                elif n == "cT":
                    pe.wait_ge(c_in, 16 * c + 16)
                elif n == "kT":
                    pe.wait_ge(kn_done, c + 1)
                elif n == "qT":
                    pe.wait_ge(qn_done, c + 1)
                elif n[:2] == "kS":
                    pe.wait_ge(kdup_done, 2 * CB * c + 2 * (int(n[2:]) + 1))
                    pe.wait_ge(klo_done, CB * c + int(n[2:]) + 1)
                elif n[:2] == "qS":
                    b = int(n[2:])
                    pe.wait_ge(qdup_done, 2 * CB * c + 2 * (b + 1))
                    for g in (2, 3):
                        pe.wait_ge(score_free[score_bank("max", b, g)], score_before(c, "max", b, g) + 1)
                elif n[:2] == "pv":
                    b = int(n[2:])
                    for g in (2, 3):
                        pe.wait_ge(score_free[score_bank("sc", b, g)], score_before(c, "sc", b, g) + 1)
                    pe.wait_ge(va_done, 2 * CB * c + 2 * (b + 1))
                elif n == "x2T":
                    pe.wait_ge(xn2_done, c + 1)
                elif n == "wT":
                    pe.wait_ge(cst_done, c + 1)
                pe.wait_ge(mix_free, mix_before(ph, n))
                if n == "xT":
                    for b in range(CB):
                        last = turn(mix[:, b * P:(b + 1) * P], xn[:, b, :], P)
                elif n == "q":
                    for b in range(CB):
                        s = slice(b * P, (b + 1) * P)
                        last = three(mix[:, s], xh[:, s], xl[:, s], wq[:, 0, :], wq[:, 1, :])
                elif n == "cT":
                    for b in range(CB):
                        last = turn(mix[:, b * KEYS:(b + 1) * KEYS], cc[:, b, :], KEYS)
                elif n[:2] == "kv":
                    for k in range(2):
                        s = slice((2 * int(n[2:]) + k) * KEYS, (2 * int(n[2:]) + k + 1) * KEYS)
                        last = three(mix[0:KEYS, k * KVW:(k + 1) * KVW], ch[:, s], cl[:, s],
                                     wkv[:, 0, :], wkv[:, 1, :])
                elif n == "qT":
                    for b in range(CB):
                        last = turn(mix[:, b * P:(b + 1) * P], qn[:, b * D:(b + 1) * D], P)
                elif n == "kT":
                    for b in range(CB):
                        last = turn(mix[:, b * KEYS:(b + 1) * KEYS], kn[:, b * D:(b + 1) * D], KEYS)
                elif n[:2] == "kS":
                    for i in range(GROUPS):
                        src = k_st[:, int(n[2:]), HG * i:HG * (i + 1), :].rearrange("p h s -> p (h s)")
                        last = turn(mix[:, i * KEYS:(i + 1) * KEYS], src, KEYS)
                elif n[:2] == "qS":
                    for i in range(GROUPS):
                        src = q_st[:, int(n[2:]), HG * i:HG * (i + 1), :].rearrange("p h s -> p (h s)")
                        last = turn(mix[:, i * P:(i + 1) * P], src, P)
                elif n[:2] == "pv":
                    b = int(n[2:])
                    for g in range(2):
                        for h in range(VG):
                            i, j = h // 2, 2 * g + h % 2
                            last = nc.tensor.matmul(mix[0:VS, g * P:(g + 1) * P],
                                                    va[:, 0, g, h * VS:(h + 1) * VS],
                                                    probs[:, j, i, :], start=(h == 0), stop=(h == VG - 1))
                        if g == 0:
                            last.then_inc(pv_half, 1)
                elif n == "oTT":
                    for b in range(CB):
                        last = turn(mix[:, b * P:(b + 1) * P], on[:, b, :], P)
                elif n[:2] == "oT":
                    for g in range(2):
                        last = turn(mix[:, g * VS:(g + 1) * VS], oa[:, g * P:(g + 1) * P], VS)
                elif n == "proj":
                    for b in range(CB):
                        s = slice(b * P, (b + 1) * P)
                        last = three(mix[:, s], oh[:, s], ol[:, s], wp[:, 0, :], wp[:, 1, :])
                elif n == "x2T":
                    for b in range(CB):
                        last = turn(mix[:, b * P:(b + 1) * P], xn[:, b, :], P)
                elif n == "gate":
                    for b in range(CB):
                        s = slice(b * P, (b + 1) * P)
                        last = three(mix[:, b * EXPERTS:(b + 1) * EXPERTS], x2h[:, s], x2l[:, s],
                                     wg[:, 0, :], wg[:, 1, :])
                elif n == "wT":
                    for b in range(CB):
                        last = turn(mix[0:SLOT, b * P:(b + 1) * P], c_st[:, b, :], P)
                last.then_inc(mix_full, 1)

            def side(ph, n):
                pe.wait_ge(mix_free, mix_before(ph, n))
                if n == "b2":
                    pe.wait_ge(gk_done, 4)
                    ins = nc.tensor.matmul(mix[:, :], b2_s[:, :], cT[0:WR, :], start=True, stop=True)
                else:
                    e = int(n[1:])
                    ins = nc.tensor.matmul(mix[:, :], sel[0:16, e:e + 1].to_broadcast([16, P]), cT[0:16, :],
                                           start=True, stop=True)
                ins.then_inc(mix_full, 1)

            def hidden(c, t, fresh=False):
                e, f = divmod(t, FB)
                for k, (bank_, full, free) in enumerate([(up[t % 2], up_full, sil_done),
                                                         (gt[t % 2], gt_full, h_done)]):
                    if not fresh or t >= 2:
                        pe.wait_ge(free, units(c, t - 1))
                    s = slice(k * FF + f * P, k * FF + (f + 1) * P)
                    three(bank_[:, :], w_hi[:, e, s], w_lo[:, e, s], x2h[:, :], x2l[:, :]).then_inc(full, 1)

            def down(ph, t):
                c, (e, f) = ph.ffn, divmod(t, FB)
                pe.wait_ge(hl_done, units(c, t + 1))
                if f == 0:
                    pe.wait_ge(y_free, y_reads(c, e))
                s = slice(2 * FF + f * P, 2 * FF + (f + 1) * P)
                three(y[:, :], w_hi[:, e, s], w_lo[:, e, s], hh[:, t % PB, :], hl[:, t % PB, :],
                      start=(f == 0), stop=(f == FB - 1)).then_inc(y_part, 1)

            def ffn(ph, s):
                if s + LAG < UNITS:
                    hidden(ph.ffn, s + LAG)
                elif ph.attn is not None:
                    if s + LAG == UNITS:
                        pe.wait_ge(mix_free, mix_at(ph, "x2T"))
                    hidden(ph.attn, s + LAG - UNITS)
                for late in (0, 1):
                    if late:
                        down(ph, s)
                    for n in due(ph, "pe", s, late):
                        (side if n in SIDE else attn)(ph, n)

            def finish(ph):
                pe.wait_ge(acc_done, EXPERTS * ph.ffn + EXPERTS)
                for b in range(CB):
                    last = turn(y[:, b * P:(b + 1) * P], acc[:, b * P:(b + 1) * P], P)
                last.then_inc(f_full, 1)

            ph = first_phase()
            for _, n in steps_of("pe"):
                attn(ph, n)
            pe.wait_ge(w_lo_done, EXPERTS)
            for t in range(LAG):
                hidden(0, t, fresh=True)
            with pe.Fori(0, CHUNKS - 1) as i:
                ph = middle_phase(i)
                for s in range(UNITS):
                    ffn(ph, s)
                finish(ph)
            ph = last_phase()
            for s in range(UNITS):
                ffn(ph, s)
            finish(ph)


def kernel(**inputs):
    import numpy as np
    import concourse.bacc as bacc
    from concourse.bass_utils import run_bass_kernel_spmd

    def blocks(a):
        return a.reshape(EXPERTS, FB, P).transpose(2, 0, 1).reshape(P, UNITS)

    sel = np.zeros((P, EXPERTS), np.float32)
    for e in range(EXPERTS):
        sel[e, e] = 1
        sel[e + EXPERTS, e] = 1
    consts = np.concatenate([
        np.eye(P, dtype=np.float32),
        (np.arange(P)[:, None] // HD % HG == np.arange(HG)[None, :]).astype(np.float32),
        np.tile(np.arange(EXPERTS, dtype=np.float32), (P, 1)),
        (np.arange(P)[:, None] < 2 * EXPERTS).astype(np.float32),
        (np.arange(P)[:, None] >= 2 * EXPERTS).astype(np.float32),
        sel], axis=1)
    laid = {n: np.ascontiguousarray(a) for n, a in inputs.items()}
    laid["L0_ffn_b1"] = np.ascontiguousarray(blocks(laid["L0_ffn_b1"]))
    laid["L0_ffn_b3"] = np.ascontiguousarray(blocks(laid["L0_ffn_b3"]))
    laid["consts"] = consts
    names = ['x', 'ctx_1024', 'g_xattn', 'g_ffn', 'L0_xattn_Wq', 'L0_xattn_Wkv', 'L0_xattn_Wproj',
             'L0_xattn_q_gamma', 'L0_xattn_k_gamma', 'L0_ffn_Wg', 'L0_ffn_bg', 'L0_ffn_W1', 'L0_ffn_b1',
             'L0_ffn_W3', 'L0_ffn_b3', 'L0_ffn_W2', 'L0_ffn_b2', 'consts']
    nc = bacc.Bacc("TRN2", target_bir_lowering=False, num_devices=1)
    f32 = mybir.dt.float32
    arrays = {f"in_{n}": laid[n] for n in names}
    args = [nc.dram_tensor(f"in_{n}", laid[n].shape, f32, kind="ExternalInput").ap() for n in names]
    out = nc.dram_tensor("out_x", (NBATCH, P, D), f32, kind="ExternalOutput").ap()
    build(nc, *args, out)
    r = run_bass_kernel_spmd(nc, [arrays], core_ids=[0])
    return r.results[0]["out_x"]
```

```python
import concourse.bass as bass
from concourse import mybir
from concourse.alu_op_type import AluOpType as ALU
from contextlib import ExitStack

P = 128
NBATCH = 16
D = 128
HEADS = 16
HD = D // HEADS
KEYS = 77
FF = 512
EXPERTS = 8
CB = 4
CHUNKS = NBATCH // CB
CT = CB * P
FB = FF // P
UNITS = EXPERTS * FB
HG = 4
GROUPS = HEADS // HG
SLOT = 32
VW = HD + 1
VG = 8
VS = VG * VW
KVW = 2 * D
LN_EPS, RMS_EPS, TOP_EPS = 1e-5, 1e-6, 1e-6
MAGIC = 0x5F3759DF

LAG = 3
HB = LAG + 1
PB = 3

AT = {
    "ln0": dict(dve=-3.2), "cT": dict(pe=-3.1, act=-3.1, dve=-3.1), "ln2": dict(dve=-2.9),
    "ln1": dict(dve=-2.8), "kv0": dict(pe=-2.1, act=-2.3), "kv1": dict(pe=-1.4, act=-0.6),
    "ksum": dict(dve=0), "xT": dict(pe=0.1, act=0, dve=0), "q": dict(pe=1.2, act=1, dve=1.4),
    "rs0": dict(dve=1.5), "rs1": dict(dve=3.6), "kn": dict(dve=4.2), "kd0": dict(pool=4.7),
    "qn": dict(dve=4.9), "qT": dict(pe=5.6, act=5.6), "klo0": dict(dve=5.6), "klo1": dict(dve=5.9),
    "kT": dict(pe=6, act=6), "kd1": dict(pool=6.3), "klo2": dict(dve=6.3), "kS0": dict(pe=6.5, act=6.6),
    "klo3": dict(dve=6.7), "kd2": dict(pool=6.8), "kb0": dict(pool=7.2), "kS1": dict(pe=7.2, act=7.7),
    "kd3": dict(pool=7.3), "mA0": dict(pe=8.7, dve=8.1), "kS2": dict(pe=8.3, act=8.2), "qlo0": dict(dve=8.4),
    "kS3": dict(pe=8.8, act=8.7), "mB0": dict(pe=9, dve=9.2), "qd0": dict(pool=9), "kb1": dict(pool=9.7),
    "qd1": dict(pool=9.8), "qS0": dict(pe=10.3, act=10), "va0": dict(pool=10.1),
    "sA0": dict(pe=10.5, act=10.3), "sB0": dict(pe=11.4, act=10.6), "kb2": dict(pool=10.6),
    "qlo1": dict(dve=11), "pv0": dict(pe=12.1, act=12.9), "mA1": dict(pe=12.1, dve=12.1),
    "va1": dict(pool=12.2), "mB1": dict(pe=12.6, dve=12.5), "qlo2": dict(dve=12.7),
    "qS1": dict(pe=13.1, act=13.2), "oT0": dict(pe=13.7, dve=13.3), "sA1": dict(pe=13.5, act=13.5),
    "sB1": dict(pe=14.4, act=13.6), "kb3": dict(pool=14.6), "qlo3": dict(dve=15),
    "mA2": dict(pe=15.5, dve=15.1), "va2": dict(pool=15.1), "qd2": dict(pool=15.2),
    "pv1": dict(pe=15.5, act=15.6), "mB2": dict(pe=15.6, dve=15.8), "qS2": dict(pe=16.1, act=16.1),
    "sA2": dict(pe=16.5, act=16.2), "oT1": dict(pe=16.6, dve=16.6), "sB2": dict(pe=17.3, act=16.7),
    "mA3": dict(pe=17.5, dve=18.1), "pv2": dict(pe=18, act=18.3), "mB3": dict(pe=18.6, dve=18.6),
    "qd3": dict(pool=19.2), "qS3": dict(pe=19.5, act=20.2), "va3": dict(pool=19.7),
    "oT2": dict(pe=20.4, dve=20.2), "sA3": dict(pe=20.4, act=20.3), "sB3": dict(pe=21.1, act=20.6),
    "pv3": dict(pe=22.2, act=22.3), "oT3": dict(pe=22.6, dve=22.6), "oTT": dict(pe=23.1, act=23.1, dve=23.4),
    "proj": dict(pe=24.3, dve=24), "nrm": dict(dve=24.7), "ln3": dict(dve=25.7),
    "x2T": dict(pe=28.2, act=28.2, dve=28.2), "gate": dict(pe=28.8, act=28.8, dve=28.8),
}
SIDE = {
    "top": dict(dve=0.2), "comb": dict(dve=1.5), "wT": dict(pe=3.1, act=2.7), "w0": dict(pe=3.9, act=3.3),
    "y0": dict(dve=3.5, pool=4.5), "w1": dict(pe=4.5, act=4.8), "b2": dict(pe=5.6, act=5.3),
    "y1": dict(dve=7.6, pool=8.5), "w2": dict(pe=9.5, act=9.5), "w3": dict(pe=10.7, act=10.5),
    "y2": dict(dve=10.7, pool=11.7), "w4": dict(pe=14.2, act=14.2), "y3": dict(dve=15.9, pool=17.7),
    "w5": dict(pe=18.9, act=18.9), "y4": dict(dve=19.4, pool=20.3), "w6": dict(pe=20.8, act=20.9),
    "y5": dict(dve=23.5, pool=24.5), "w7": dict(pe=26.4, act=26.4), "y6": dict(dve=27.6, pool=28.4),
    "fin": dict(pe=31.99),
}
FIRST_ORDER = {
    "pe": (
        [
            "cT", "kv0", "kv1",
        ], [
            "warm3", "xT", "warm1", "q", "warm13", "qT", "kT", "warm1", "kS0", "kS1", "kS2", "mA0", "kS3",
            "mB0", "warm1", "qS0", "warm1", "sA0", "warm2", "sB0", "warm2", "mA1", "pv0", "mB1", "warm2",
            "qS1", "warm2", "sA1", "oT0", "sB1", "warm2", "mA2", "pv1", "mB2", "warm1", "qS2", "warm2",
            "oT1", "warm1", "mA3", "sA2", "warm1", "sB2", "warm1", "pv2", "mB3", "warm3", "qS3", "sA3",
            "warm1", "oT2", "sB3", "warm1", "pv3", "warm1", "oT3", "warm1", "oTT", "proj", "warm8", "x2T",
            "gate",
        ]),
    "act": (
        [
            "cT", "hi0", "kv0", "hi1", "kv1",
        ], [
            "xT", "hi2", "q", "hi3", "qT", "kT", "kS0", "kS1", "kS2", "kS3", "hi4", "qS0", "sA0", "sB0",
            "pv0", "hi5", "qS1", "sA1", "sB1", "pv1", "qS2", "hi6", "sA2", "sB2", "hi7", "pv2", "qS3", "sA3",
            "sB3", "pv3", "oTT", "x2T", "gate",
        ]),
    "dve": (
        [
            "ln0", "cT", "ln1", "ln2",
        ], [
            "xT", "ksum", "q", "rs0", "rs1", "kn", "qn", "klo0", "klo1", "klo2", "klo3", "mA0", "qlo0",
            "qlo1", "mB0", "mA1", "mB1", "oT0", "qlo3", "qlo2", "mA2", "mB2", "oT1", "mA3", "mB3", "oT2",
            "oT3", "oTT", "proj", "nrm", "ln3", "x2T", "gate",
        ]),
    "pool": (
        [
            "lo0", "lo1", "lo2",
        ], [
            "kd0", "kd1", "kd2", "kd3", "kb0", "lo3", "kb1", "va0", "qd0", "lo4", "kb2", "qd1", "qd2", "kb3",
            "va1", "va2", "lo5", "lo6", "qd3", "lo7", "va3",
        ]),
}
ALL_MIX = ["cT", "kv0", "kv1", "xT", "q", "qT", "kT", "oTT", "proj", "x2T", "gate", "wT", "b2", "fin"] + \
    [f"w{e}" for e in range(EXPERTS)] + \
    [f"{n}{b}" for n in ("kS", "qS", "pv", "oT") for b in range(CB)]


FRONT = [n for n, t in AT.items() if min(t.values()) < 0]
FRONT_SLOT = UNITS - 4


def steps_of(engine, attn=True, front=True, ffn=False):
    table = [(t[engine], n) for n, t in AT.items() if engine in t and attn and n not in FRONT]
    table += [(t[engine] + UNITS, n) for n, t in AT.items() if engine in t and front and n in FRONT]
    table += [(t[engine], n) for n, t in SIDE.items() if engine in t and ffn]
    return sorted(table)


def first_steps(engine, front):
    return FIRST_ORDER[engine][0 if front else 1]


def due(ph, engine, slot, late):
    first = slot + 0.5 * late
    steps = steps_of(engine, ph.attn is not None and ph.ffn is not None, ph.front is not None, ph.ffn is not None)
    return [n for t, n in steps if first <= t + 1e-9 < first + 0.5]


UNIT_GROUPS = {"mA": range(0, 2), "mB": range(2, 4), "sA": range(0, 2), "sB": range(2, 4)}

def mix_order(**parts):
    return [n for _, n in steps_of("pe", **parts) if n in ALL_MIX]


START = [n for n in first_steps("pe", True) if n in ALL_MIX]
ALONE = [n for n in first_steps("pe", False) if n in ALL_MIX] + mix_order(attn=False)
BOTH = mix_order(ffn=True)
LATE = mix_order(front=False, ffn=True)
LAST = mix_order(attn=False, front=False, ffn=True)
def score_order(steps):
    order = {}
    for n in steps:
        for g in UNIT_GROUPS.get(n[:-1], ()):
            order[("max" if n[0] == "m" else "sc", int(n[-1]), g)] = len(order)
    return order


SCORE_FIRST = score_order(first_steps("pe", False))
SCORE = score_order([n for _, n in steps_of("pe", front=False)])
NSCORE = len(SCORE) // 2
FRONT_LINKS, REST_LINKS, ROUTE_LINKS = 14, 34, 13
LINKS = FRONT_LINKS + REST_LINKS + ROUTE_LINKS


class Phase:

    def __init__(self, attn, ffn, front, base, order, links):
        self.attn, self.ffn, self.front = attn, ffn, front
        self.base, self.order, self.links = base, order, links


def start_phase():
    return Phase(None, None, 0, 0, START, 0)


def first_phase():
    return Phase(0, None, 1, len(START), ALONE, FRONT_LINKS)


def middle_phase(i):
    return Phase(i + 1, i, i + 2, i * len(BOTH) + len(START) + len(ALONE), BOTH,
                 2 * FRONT_LINKS + REST_LINKS + i * LINKS)


def late_phase():
    ph = middle_phase(CHUNKS - 2)
    return Phase(CHUNKS - 1, CHUNKS - 2, None, ph.base, LATE, ph.links)


def last_phase():
    return Phase(None, CHUNKS - 1, None, late_phase().base + len(LATE), LAST,
                 late_phase().links + REST_LINKS + ROUTE_LINKS)


def build(nc, x, ctx_in, gx, gf, Wq, Wkv, Wproj, qg, kg, Wg, bg, W1, b1, W3, b3, W2, b2, consts, out):
    f32, f32r = mybir.dt.float32, mybir.dt.float32r
    i32, u32 = mybir.dt.int32, mybir.dt.uint32
    ACT, AX = mybir.ActivationFunctionType, mybir.AxisListType

    with ExitStack() as stack:
        def sb(name, shape, dt=f32):
            return stack.enter_context(nc.sbuf_tensor(name, shape, dt))

        def sem(name):
            return stack.enter_context(nc.semaphore(name))

        NCONST = consts.shape[1]
        cst = sb("cst", [P, NCONST])
        ident = cst[:, 0:P]
        hmask = cst[:, P:P + HG]
        iota = cst[:, P + HG:P + HG + EXPERTS]
        is_hi = cst[0:3 * EXPERTS, P + HG + EXPERTS:P + HG + EXPERTS + 1]
        is_lo = cst[0:3 * EXPERTS, P + HG + EXPERTS + 1:P + HG + EXPERTS + 2]
        sel_raw = cst[0:SLOT, P + HG + EXPERTS + 2:NCONST]
        sel = sb("sel", [SLOT, EXPERTS], f32r)
        acc = sb("acc", [P, CT])
        wq_raw, wp_raw, wkv_raw = acc[:, 0:D], acc[:, D:2 * D], acc[:, 2 * D:2 * D + KVW]
        wg_raw = sb("wg_raw", [D, EXPERTS])
        wq = sb("wq", [D, 2, D], f32r)
        wp = sb("wp", [D, 2, D], f32r)
        wkv = sb("wkv", [D, 2, KVW], f32r)
        wg = sb("wg", [D, 2, EXPERTS], f32r)
        EW = 3 * FF
        w_hi = sb("w_hi", [P, EXPERTS, EW], f32r)
        w_lo = sb("w_lo", [P, EXPERTS, EW], f32r)
        b1_sb, b3_sb = sb("b1_sb", [P, UNITS]), sb("b3_sb", [P, UNITS])
        bg_sb = sb("bg_sb", [P, EXPERTS])
        WR = 3 * EXPERTS
        b2_raw, b2_d = sb("b2_raw", [WR, D]), sb("b2_d", [WR, D])
        b2_hi, b2_s = sb("b2_hi", [WR, D], f32r), sb("b2_s", [WR, D], f32r)
        gates = sb("gates", [P, 2])
        gk = sb("gk", [KEYS, HD])
        gq = sb("gq", [KEYS, HD])

        xc = sb("xc", [P, CB, D])
        cc = sb("cc", [KEYS, CB, D])
        x1 = sb("x1", [P, 2 * CT])
        pad, one = sb("pad", [P, 1]), sb("one", [P, 1])
        stats = sb("stats", [P, CB, 6])
        mv = sb("mv", [P, CB, 2])
        xn = sb("xn", [P, CB, D])
        xh, xl = sb("xh", [D, CT], f32r), sb("xl", [D, CT], f32r)
        qr, sq = sb("qr", [P, CT]), xn[:, :, :].rearrange("p b d -> p (b d)")
        on = sb("on", [P, CB, D])
        kvr, ksq = sb("kvr", [KEYS, CB, KVW]), on[0:KEYS, :, :]
        NR = CB * HEADS
        ss = sb("ss", [P, 2 * NR])
        nt1, nt2, rinv = sb("nt1", [P, 2 * NR]), sb("nt2", [P, 2 * NR]), sb("rinv", [P, 2 * NR])
        qn, qhi = sb("qn", [P, CT]), sq.bitcast(f32r)
        kn, khi = sb("kn", [KEYS, CT]), on[0:KEYS, :, :].rearrange("p b d -> p (b d)").bitcast(f32r)
        q_st = sb("q_st", [P, CB, HEADS, SLOT])
        k_st = q_st[0:KEYS]
        qTh = sb("qTh", [D, CT], f32r)
        kT = qr[:, 0:CB * KEYS]
        k_bd = sb("k_bd", [D, CB, HG, KEYS], f32r)
        ksT = sb("ksT", [P, CB, GROUPS, KEYS], f32r)
        ch, cl = (ksT[:, b, :, :].rearrange("p i t -> p (i t)") for b in range(2))
        qsT = sb("qsT", [P, 2, GROUPS, P], f32r)
        probs = sb("probs", [KEYS, HG, GROUPS, P])
        va = sb("va", [KEYS, 2, VG * (VS + VW)])
        oa = sb("oa", [VS, 2 * P])
        rden = sb("rden", [P, HEADS])
        oh, ol = xh, xl
        x2h, x2l = sb("x2h", [D, CT], f32r), sb("x2l", [D, CT], f32r)
        lg, ex, pr = sb("lg", [P, CB, EXPERTS]), sb("ex", [P, CB, EXPERTS]), sb("pr", [P, CB, EXPERTS])
        r4, s4 = sb("r4", [P, CB]), sb("s4", [P, CB])
        top = sb("top", [P, CB, 8])
        topi = sb("topi", [P, CB, 8], u32)
        topf = sb("topf", [P, CB, 8])
        e12, e1 = sb("e12", [P, CB, 2, EXPERTS]), sb("e1", [P, CB, EXPERTS])
        chi = sb("chi", [P, CB, EXPERTS], f32r)
        c_st = sb("c_st", [P, CB, SLOT])
        cT = sb("cT", [SLOT, CT], f32r)
        cbc = sb("cbc", [P, 2, CT])
        arena = sb("arena", [P, 2 * EW])
        w_raw = arena[:, :].rearrange("p (k w) -> p k w", k=2)
        hf = arena[:, 0:HB * CT].rearrange("p (k t) -> p k t", k=HB)
        yt = arena[:, HB * CT:(HB + 2) * CT].rearrange("p (k t) -> p k t", k=2)
        outb = yt[:, 0, :]
        hh, hl = sb("hh", [P, PB, CT], f32r), sb("hl", [P, PB, CT], f32r)

        def bank(name):
            return stack.enter_context(nc.psum_tensor(name, [P, 512], f32))

        up, gt = [bank("up0"), bank("up1")], [bank("gt0"), bank("gt1")]
        y = bank("y")
        score = [bank("score0"), bank("score1")]
        mix = bank("mix")

        cst_in, small_in, bias_in = sem("cst_in"), sem("small_in"), sem("bias_in")
        w_in = [sem("w_in0"), sem("w_in1")]
        outb_free = sem("outb_free")
        x_in, c_in, out_done = sem("x_in"), sem("c_in"), sem("out_done")
        small_hi, small_lo = sem("small_hi"), sem("small_lo")
        w_hi_done, w_lo_done = sem("w_hi_done"), sem("w_lo_done")
        init_done, tanh_done, b2_hi_done = sem("init_done"), sem("tanh_done"), sem("b2_hi_done")
        gk_done, va_zero = sem("gk_done"), sem("va_zero")
        link_s = sem("link_s")
        mix_full, mix_free = sem("mix_full"), sem("mix_free")
        score_full = sem("score_full")
        score_free = [sem("score_free0"), sem("score_free1")]
        xn_done, xh_done, ch_done = sem("xn_done"), sem("xh_done"), sem("ch_done")
        qsq_done, ksq_done = sem("qsq_done"), sem("ksq_done")
        qn_done, kn_done, qhi_done, khi_done = sem("qn_done"), sem("kn_done"), sem("qhi_done"), sem("khi_done")
        qdup_done, kdup_done, klo_done = sem("qdup_done"), sem("kdup_done"), sem("klo_done")
        kbd_done, va_done = sem("kbd_done"), sem("va_done")
        pv_half = sem("pv_half")
        shift_done, on_done, oh_done, x1_done = sem("shift_done"), sem("on_done"), sem("oh_done"), sem("x1_done")
        xn2_done, x2h_done = sem("xn2_done"), sem("x2h_done")
        lg_done, ex_done, cst_done = sem("lg_done"), sem("ex_done"), sem("cst_done")
        up_full, gt_full = sem("up_full"), sem("gt_full")
        sil_done, h_done, hh_done, hl_done = sem("sil_done"), sem("h_done"), sem("hh_done"), sem("hl_done")
        y_part, y_free, acc_done = sem("y_part"), sem("y_free"), sem("acc_done")

        block = stack.enter_context(nc.Block())

        def chunk_of(ph, name):
            return ph.front if name in FRONT else ph.attn

        def mix_at(ph, name):
            return ph.base + (ph.order.index(name) + 1)

        def mix_before(ph, name):
            return ph.base + ph.order.index(name)

        def score_place(ph, kind, b, g):
            return (SCORE_FIRST if ph.ffn is None else SCORE)[(kind, b, g)]

        def score_at(ph, kind, b, g):
            return len(SCORE) * ph.attn + score_place(ph, kind, b, g) + 1

        def score_bank(ph, kind, b, g):
            return score_place(ph, kind, b, g) % 2

        def score_before(ph, kind, b, g):
            return NSCORE * ph.attn + score_place(ph, kind, b, g) // 2

        def y_reads(c, n):
            return EXPERTS * c + n + 1

        def adds(c, n):
            return (EXPERTS - 1) * c + n

        def units(c, n):
            return UNITS * c + n

        def x1_chunk(c):
            return x1[:, bass.ds((c % 2) * CT, CT)]

        @block.sync
        def _(sp):
            def load(c):
                sp.dma_start(xc[:, :, :], x[bass.ds(c * CB, CB), :, :].rearrange("b p d -> p b d")).then_inc(x_in, 16)
                sp.dma_start(cc[:, :, :], ctx_in[bass.ds(c * CB, CB), :, :].rearrange("b p d -> p b d")).then_inc(c_in, 16)

            load(0)
            sp.dma_start(cst[:, :], consts).then_inc(cst_in, 16)
            sp.dma_start(wq_raw[:, :], Wq).then_inc(small_in, 16)
            sp.dma_start(wkv_raw[:, :], Wkv).then_inc(small_in, 16)
            sp.dma_start(wp_raw[:, :], Wproj).then_inc(small_in, 16)
            sp.dma_start(wg_raw[:, :], Wg).then_inc(small_in, 16)
            def load_biases():
                sp.dma_start(gates[:, 0:1], gx.partition_broadcast(P)).then_inc(bias_in, 16)
                sp.dma_start(gates[:, 1:2], gf.partition_broadcast(P)).then_inc(bias_in, 16)
                sp.dma_start(gq[:, :], qg.partition_broadcast(KEYS)).then_inc(bias_in, 16)
                sp.dma_start(gk[:, :], kg.partition_broadcast(KEYS)).then_inc(bias_in, 16)
                sp.dma_start(bg_sb[:, :], bg.partition_broadcast(P)).then_inc(bias_in, 16)
                sp.dma_start(b1_sb[:, :], b1).then_inc(bias_in, 16)
                sp.dma_start(b3_sb[:, :], b3).then_inc(bias_in, 16)
                for k in range(3):
                    sp.dma_start(b2_raw[EXPERTS * k:EXPERTS * (k + 1), :], b2).then_inc(bias_in, 16)

            def load_weights():
                for e in range(EXPERTS):
                    if e == 2:
                        load_biases()
                    if e >= 2:
                        sp.wait_ge(w_hi_done, e - 1)
                        sp.wait_ge(w_lo_done, e - 1)
                    dst = w_raw[:, e % 2, :]
                    sp.dma_start(dst[:, 0:FF], W1[e, :, :]).then_inc(w_in[e % 2], 16)
                    sp.dma_start(dst[:, FF:2 * FF], W3[e, :, :]).then_inc(w_in[e % 2], 16)
                    sp.dma_start(dst[:, 2 * FF:EW].rearrange("p (f d) -> p f d", f=FB),
                                 W2[e, :, :].rearrange("(f p) d -> p f d", p=P)).then_inc(w_in[e % 2], 16)

            def store(ph):
                c = ph.ffn
                sp.wait_ge(mix_free, mix_at(ph, "fin"))
                sp.dma_start(out[bass.ds(c * CB, CB), :, :].rearrange("b p d -> p b d"),
                             outb.rearrange("p (b d) -> p b d", b=CB)).then_inc(out_done, 16)
                sp.wait_ge(out_done, 16 * c + 16)
                sp.sem_inc(outb_free, 1)

            load_weights()
            sp.wait_ge(x1_done, 1)
            load(1)
            with sp.Fori(0, CHUNKS - 2) as i:
                sp.wait_ge(x1_done, i + 2)
                load(i + 2)
                store(middle_phase(i))
            store(late_phase())
            store(last_phase())

        @block.gpsimd
        def _(pool):
            def same(dst, src):
                ones = one[0:src.shape[0], :]
                while len(ones.shape) < len(src.shape):
                    ones = ones.unsqueeze(1)
                return nc.gpsimd.tensor_tensor(dst, src, ones.to_broadcast(list(src.shape)), ALU.mult)

            def split(e):
                pool.wait_ge(w_hi_done, e + 1)
                nc.gpsimd.tensor_tensor(w_lo[:, e, :], w_raw[:, e % 2, :], w_hi[:, e, :].bitcast(f32),
                                        ALU.subtract).then_inc(w_lo_done, 1)

            def heads(ap):
                return ap.rearrange("p (h d) -> p h d", d=HD)

            def attn(ph, n):
                c, b = chunk_of(ph, n), int(n[-1])
                if n[:2] == "kd":
                    pool.wait_ge(khi_done, c + 1)
                    src = heads(khi[:, b * D:(b + 1) * D].bitcast(f32))
                    same(k_st[:, b, :, 0:HD], src).then_inc(kdup_done, 1)
                    same(k_st[:, b, :, HD:2 * HD], src).then_inc(kdup_done, 1)
                elif n[:2] == "kb":
                    pool.wait_ge(mix_free, mix_at(ph, "kT"))
                    nc.gpsimd.tensor_tensor(
                        k_bd[:, b, :, :], kT[:, b * KEYS:(b + 1) * KEYS].unsqueeze(1).to_broadcast([D, HG, KEYS]),
                        hmask.unsqueeze(2).to_broadcast([D, HG, KEYS]), ALU.mult).then_inc(kbd_done, 1)
                elif n[:2] == "va":
                    if b == 0:
                        pool.wait_ge(mix_free, ph.base)
                    else:
                        pool.wait_ge(mix_full, mix_at(ph, f"pv{b - 1}"))
                    for g in range(2):
                        src = kvr[:, b, D:2 * D].rearrange("p (i g j d) -> p i g j d", i=GROUPS, g=2, d=HD)[:, :, g]
                        dst = va[:, g, :].rearrange("p (i j s) -> p i j s", i=GROUPS, j=2)[:, :, :, 0:HD]
                        same(dst, src).then_inc(va_done, 1)
                elif n[:2] == "qd":
                    pool.wait_ge(mix_full, mix_at(ph, "kS3"))
                    pool.wait_ge(qhi_done, c + 1)
                    src = heads(qhi[:, b * D:(b + 1) * D].bitcast(f32))
                    same(q_st[:, b, :, 0:HD], src).then_inc(qdup_done, 1)
                    same(q_st[:, b, :, 2 * HD:3 * HD], src).then_inc(qdup_done, 1)

            def low(c, t):
                pool.wait_ge(hh_done, units(c, t + 1))
                nc.gpsimd.tensor_tensor(hl[:, t % PB, :], hf[:, t % HB, :], hh[:, t % PB, :].bitcast(f32),
                                        ALU.subtract).then_inc(hl_done, 1)

            def add_y(ph, e):
                c = ph.ffn
                pool.wait_ge(y_free, y_reads(c, e + 1))
                if e == 0:
                    pool.wait_ge(mix_free, mix_at(ph, "b2"))
                else:
                    pool.wait_ge(acc_done, adds(c, e))
                nc.gpsimd.tensor_tensor(acc[:, :], acc[:, :], yt[:, e % 2, :], ALU.add).then_inc(acc_done, 1)

            def ffn(ph, s):
                for late in (0, 1):
                    if late:
                        t = s + LAG - 1
                        if t >= UNITS and ph.attn is not None:
                            low(ph.attn, t - UNITS)
                        elif t < UNITS and ph.ffn is not None:
                            low(ph.ffn, t)
                    for n in due(ph, "pool", s, late):
                        if n in SIDE:
                            add_y(ph, int(n[1:]))
                        else:
                            attn(ph, n)

            nc.gpsimd.memset(one[:, :], 1.0)
            nc.gpsimd.memset(q_st[:, :, :, :], 0.0).then_inc(init_done, 1)
            nc.gpsimd.memset(va[:, :, :], 0.0).then_inc(va_zero, 1)
            pool.wait_ge(va_zero, 1)
            for g in range(2):
                nc.gpsimd.memset(va[:, g, :].rearrange("p (h s) -> p h s", h=VG)[:, :, HD:HD + 1], 1.0)
            nc.gpsimd.memset(c_st[:, :, :], 0.0).then_inc(init_done, 1)
            ph = first_phase()
            for n in first_steps("pool", True) + first_steps("pool", False):
                if n[:2] == "lo":
                    split(int(n[2:]))
                else:
                    attn(ph, n)
            for s in range(FRONT_SLOT, UNITS):
                ffn(ph, s)
            with pool.Fori(0, CHUNKS - 2) as i:
                ph = middle_phase(i)
                for s in range(UNITS):
                    ffn(ph, s)
            for ph in (late_phase(), last_phase()):
                for s in range(UNITS):
                    ffn(ph, s)

        @block.scalar
        def _(act):
            act.wait_ge(small_in, 64)
            nc.scalar.copy(wq[:, 0, :], wq_raw[:, :]).then_inc(small_hi, 1)
            nc.scalar.copy(wkv[:, 0, :], wkv_raw[:, :]).then_inc(small_hi, 1)
            nc.scalar.copy(wp[:, 0, :], wp_raw[:, :]).then_inc(small_hi, 1)
            nc.scalar.copy(wg[:, 0, :], wg_raw[:, :]).then_inc(small_hi, 1)
            act.wait_ge(cst_in, 16)
            nc.scalar.copy(sel[:, :], sel_raw).then_inc(small_hi, 1)

            def split(e):
                act.wait_ge(w_in[e % 2], 48 * (e // 2 + 1))
                nc.scalar.copy(w_hi[:, e, :], w_raw[:, e % 2, :]).then_inc(w_hi_done, 1)

            def attn(ph, n):
                c = chunk_of(ph, n)
                if n[:2] in ("sA", "sB"):
                    b = int(n[2:])
                    for j in UNIT_GROUPS[n[:2]]:
                        k = score_bank(ph, "sc", b, j)
                        act.wait_ge(score_full, score_at(ph, "sc", b, j))
                        if b >= 1 and j == 0:
                            act.wait_ge(pv_half, CB * c + b)
                        if b >= 1 and j == 2:
                            act.wait_ge(mix_full, mix_at(ph, f"pv{b - 1}"))
                        nc.scalar.activation(probs[:, j, :, :].rearrange("p i t -> p (i t)"),
                                             score[k][0:KEYS, :], ACT.Exp).then_inc(score_free[k], 1)
                    return
                if n == "gate":
                    act.wait_ge(lg_done, c + 1)
                    nc.scalar.activation(ex[:, :, :], lg[:, :, :], ACT.Exp).then_inc(ex_done, 1)
                    return
                act.wait_ge(mix_full, mix_at(ph, n))
                if n == "xT":
                    nc.scalar.copy(xh[:, :], mix[:, :]).then_inc(xh_done, 1)
                elif n == "q":
                    nc.scalar.activation(sq[:, :], mix[:, :], ACT.Square).then_inc(qsq_done, 1)
                    nc.scalar.copy(qr[:, :], mix[:, :]).then_inc(mix_free, 1)
                elif n == "cT":
                    nc.scalar.copy(ch[:, :], mix[:, 0:CB * KEYS]).then_inc(ch_done, 1)
                elif n[:2] == "kv":
                    a = 2 * int(n[2:])
                    src = mix[0:KEYS, :].rearrange("p (b w) -> p b w", b=2)
                    nc.scalar.activation(ksq[:, a:a + 2, :], src[:, :, 0:D], ACT.Square).then_inc(ksq_done, 1)
                    nc.scalar.copy(kvr[:, a:a + 2, :], src).then_inc(mix_free, 1)
                elif n == "qT":
                    nc.scalar.copy(qTh[:, :], mix[:, :]).then_inc(mix_free, 1)
                elif n == "kT":
                    nc.scalar.copy(kT[:, :], mix[:, 0:CB * KEYS]).then_inc(mix_free, 1)
                elif n[:2] == "kS":
                    b = int(n[2:])
                    nc.scalar.copy(ksT[:, b, :, :].rearrange("p i t -> p (i t)"),
                                   mix[:, 0:GROUPS * KEYS]).then_inc(mix_free, 1)
                elif n[:2] == "qS":
                    b = int(n[2:])
                    nc.scalar.copy(qsT[:, b % 2, :, :].rearrange("p i t -> p (i t)"),
                                   mix[:, :]).then_inc(mix_free, 1)
                elif n[:2] == "pv":
                    nc.scalar.copy(oa[:, :], mix[0:VS, 0:2 * P]).then_inc(mix_free, 1)
                elif n == "oTT":
                    nc.scalar.copy(oh[:, :], mix[:, :]).then_inc(oh_done, 1)

                elif n == "x2T":
                    act.wait_ge(gt_full, UNITS * c)
                    nc.scalar.copy(x2h[:, :], mix[:, :]).then_inc(x2h_done, 1)

            def spread(ph, n):
                act.wait_ge(mix_full, mix_at(ph, n))
                if n == "wT":
                    nc.scalar.copy(cT[:, :], mix[0:SLOT, :]).then_inc(mix_free, 1)
                    return
                if n == "b2":
                    nc.scalar.copy(acc[:, :], mix[:, :]).then_inc(mix_free, 1)
                    return
                e = int(n[1:])
                if e >= 2:
                    act.wait_ge(y_free, y_reads(ph.ffn, e - 1))
                nc.scalar.copy(cbc[:, e % 2, :], mix[:, :]).then_inc(mix_free, 1)

            def silu(c, t, fresh=False):
                act.wait_ge(up_full, units(c, t + 1))
                if not fresh:
                    act.wait_ge(hl_done, units(c, 1 if t == LAG else t + 1 - HB))
                nc.scalar.activation(hf[:, t % HB, :], up[t % 2][:, :], ACT.Silu,
                                     bias=b1_sb[:, t:t + 1]).then_inc(sil_done, 1)

            def high(c, t, fresh=False):
                act.wait_ge(h_done, units(c, t + 1))
                if t >= PB:
                    act.wait_ge(y_part, units(c, t + 1 - PB))
                elif t < 2 and not fresh:
                    act.wait_ge(y_part, units(c, t - 1))
                nc.scalar.copy(hh[:, t % PB, :], hf[:, t % HB, :]).then_inc(hh_done, 1)

            def ffn(ph, s):
                c, nxt = ph.ffn, ph.attn
                for late in (0, 1):
                    for part, t in ((high, s + LAG - 1),) if late else ((silu, s + LAG),):
                        if t >= UNITS and nxt is not None:
                            part(nxt, t - UNITS, fresh=c is None)
                        elif t < UNITS and c is not None:
                            part(c, t)
                    for n in due(ph, "act", s, late):
                        (spread if n in SIDE else attn)(ph, n)

            for ph, front in ((start_phase(), True), (first_phase(), False)):
                for n in first_steps("act", front):
                    if n[:2] == "hi":
                        split(int(n[2:]))
                    else:
                        attn(ph, n)
                if front:
                    act.wait_ge(bias_in, 160)
                    nc.scalar.activation(gates[:, :], gates[:, :], ACT.Tanh).then_inc(tanh_done, 1)
                    nc.scalar.copy(b2_hi[:, :], b2_raw[:, :]).then_inc(b2_hi_done, 1)
            act.wait_ge(w_lo_done, EXPERTS)
            for s in range(FRONT_SLOT, UNITS):
                ffn(first_phase(), s)
            with act.Fori(0, CHUNKS - 2) as i:
                ph = middle_phase(i)
                for s in range(UNITS):
                    ffn(ph, s)
            for ph in (late_phase(), last_phase()):
                for s in range(UNITS):
                    ffn(ph, s)

        @block.vector
        def _(dve):
            ve = nc.vector
            ve.memset(pad[:, :], 0.0).then_inc(outb_free, 1)
            ve.memset(rden[:, :], 0.0).then_inc(y_free, 1)
            ve.memset(ss[:, :], 1.0).then_inc(init_done, 1)

            def biases():
                dve.wait_ge(bias_in, 160)
                dve.wait_ge(cst_in, 16)
                dve.wait_ge(init_done, 3)
                ve.scalar_tensor_tensor(out=gk[:, :], in0=gk[:, :], scalar=float(HD) ** -0.5, in1=gq[:, :],
                                        op0=ALU.mult, op1=ALU.mult).then_inc(gk_done, 1)
                dve.wait_ge(b2_hi_done, 1)
                ve.tensor_tensor(b2_d[:, :], b2_raw[:, :], b2_hi[:, :].bitcast(f32), ALU.subtract).then_inc(gk_done, 1)
                dve.wait_ge(gk_done, 2)
                ve.tensor_scalar(b2_raw[:, :], b2_hi[:, :].bitcast(f32), is_hi, None, ALU.mult).then_inc(gk_done, 1)
                dve.wait_ge(gk_done, 3)
                ve.scalar_tensor_tensor(out=b2_s[:, :], in0=b2_d[:, :], scalar=is_lo, in1=b2_raw[:, :],
                                        op0=ALU.mult, op1=ALU.add).then_inc(gk_done, 1)

            def small_parts():
                for k, (raw, hi, lo) in enumerate([(wq_raw[:, :], wq[:, 0, :], wq[:, 1, :]),
                                                   (wkv_raw[:, :], wkv[:, 0, :], wkv[:, 1, :]),
                                                   (wp_raw[:, :], wp[:, 0, :], wp[:, 1, :]),
                                                   (wg_raw[:, :], wg[:, 0, :], wg[:, 1, :])]):
                    dve.wait_ge(small_hi, k + 1)
                    ve.tensor_tensor(lo, raw, hi.bitcast(f32), ALU.subtract).then_inc(small_lo, 1)

            links, phase_links = [0], [0]

            def enter(ph):
                links[0], phase_links[0] = 0, ph.links
                return ph

            def link(c, ins):
                links[0] += 1
                ins.then_inc(link_s, 1)
                dve.wait_ge(link_s, phase_links[0] + links[0])

            def hold():
                return ve.memset(pad[:, :], 0.0)

            def guess(c, v, dst, t1):
                link(c, ve.tensor_scalar(t1.bitcast(i32), v.bitcast(i32), 1, None, ALU.logical_shift_right))
                ve.tensor_scalar(dst.bitcast(i32), t1.bitcast(i32), -1.0, float(MAGIC), ALU.mult, ALU.add)
                link(c, ve.tensor_scalar(v, v, -0.5, None, ALU.mult))

            def newton(c, v, dst, t1, t2, steps=3):
                for _ in range(steps):
                    link(c, ve.tensor_tensor(t1, dst, dst, ALU.mult))
                    link(c, ve.tensor_tensor(t2, t1, v, ALU.mult))
                    link(c, ve.scalar_tensor_tensor(out=dst, in0=t2, scalar=1.5, in1=dst,
                                                    op0=ALU.add, op1=ALU.mult))

            NORM = (s4[:, :], r4[:, :], nt1[:, 0:CB], nt2[:, 0:CB])

            def moments(c, src):
                for b in range(CB):
                    ins = ve.bn_stats(stats[:, b, :], src[:, b, :])
                link(c, ins)
                hold()
                for b in range(CB):
                    ins = ve.bn_aggr(mv[:, b, :], stats[:, b, :])
                link(c, ins)
                link(c, ve.tensor_scalar(s4[:, :], mv[:, :, 1], LN_EPS, None, ALU.add))
                guess(c, *NORM[0:3])

            def normed(src):
                for b in range(CB):
                    ins = ve.tensor_scalar(xn[:, b, :], src[:, b, :], mv[:, b, 0:1], r4[:, b:b + 1],
                                           ALU.subtract, ALU.mult)
                return ins

            def heads(ap):
                return ap.rearrange("p (h d) -> p h d", d=HD)

            ROOTS = (ss[:, :], rinv[:, :], nt1[:, :], nt2[:, :])

            def attn(ph, n):
                c = chunk_of(ph, n)
                if n == "ln0":
                    ve.memset(k_st[:, :, :, 3 * HD:3 * HD + 1], 1.0)
                    dve.wait_ge(x_in, 16 * c + 16)
                    hold()
                    moments(c, xc)
                elif n == "ln1":
                    newton(c, *NORM)
                elif n == "ln2":
                    normed(xc).then_inc(xn_done, 1)
                elif n == "xT":
                    dve.wait_ge(xh_done, c + 1)
                    ve.tensor_tensor(xl[:, :], mix[:, :], xh[:, :].bitcast(f32), ALU.subtract).then_inc(mix_free, 1)
                elif n == "q":
                    dve.wait_ge(qsq_done, c + 1)
                    link(c, ve.tensor_reduce(ss[:, 0:NR], heads(sq[:, :]), AX.X, ALU.add))
                    link(c, ve.tensor_scalar(ss[:, :], ss[:, :], 1.0 / HD, RMS_EPS, ALU.mult, ALU.add))
                elif n == "cT":
                    dve.wait_ge(ch_done, c + 1)
                    ve.tensor_tensor(cl[:, :], mix[:, 0:CB * KEYS], ch[:, :].bitcast(f32),
                                     ALU.subtract).then_inc(mix_free, 1)
                elif n == "ksum":
                    dve.wait_ge(ksq_done, 2 * c + 2)
                    link(c, ve.tensor_reduce(ss[0:KEYS, NR:2 * NR],
                                             heads(ksq[:, :, :].rearrange("p b d -> p (b d)")), AX.X, ALU.add))
                elif n == "rs0":
                    guess(c, *ROOTS[0:3])
                    newton(c, *ROOTS, steps=1)
                elif n == "rs1":
                    newton(c, *ROOTS, steps=2)
                elif n == "kn":
                    dve.wait_ge(mix_free, mix_at(ph, "q"))
                    rk = rinv[0:KEYS, NR:2 * NR]
                    for b in range(CB):
                        ins = ve.tensor_tensor(heads(kn[:, b * D:(b + 1) * D]), heads(kvr[:, b, 0:D]),
                                               rk[:, b * HEADS:(b + 1) * HEADS].unsqueeze(2)
                                               .to_broadcast([KEYS, HEADS, HD]), ALU.mult)
                    link(c, ins)
                    ve.tensor_tensor(heads(kn[:, :]), heads(kn[:, :]),
                                     gk[:, :].unsqueeze(1).to_broadcast([KEYS, NR, HD]), ALU.mult).then_inc(kn_done, 1)
                elif n == "qn":
                    ve.tensor_tensor(heads(qn[:, :]), heads(qr[:, :]),
                                     rinv[:, 0:NR].unsqueeze(2).to_broadcast([P, NR, HD]), ALU.mult).then_inc(qn_done, 1)
                    dve.wait_ge(kn_done, c + 1)
                    ve.tensor_copy(khi[:, :], kn[:, :]).then_inc(khi_done, 1)
                    dve.wait_ge(qn_done, c + 1)
                    ve.tensor_copy(qhi[:, :], qn[:, :]).then_inc(qhi_done, 1)
                elif n[:3] == "klo":
                    b = int(n[3:])
                    dve.wait_ge(khi_done, c + 1)
                    ve.tensor_tensor(k_st[:, b, :, 2 * HD:3 * HD], heads(kn[:, b * D:(b + 1) * D]),
                                     heads(khi[:, b * D:(b + 1) * D].bitcast(f32)),
                                     ALU.subtract).then_inc(klo_done, 1)
                elif n[:3] == "qlo":
                    b = int(n[3:])
                    dve.wait_ge(qhi_done, c + 1)
                    dve.wait_ge(mix_full, mix_at(ph, "kS3"))
                    ve.tensor_tensor(q_st[:, b, :, HD:2 * HD], heads(qn[:, b * D:(b + 1) * D]),
                                     heads(qhi[:, b * D:(b + 1) * D].bitcast(f32)), ALU.subtract)
                elif n[:2] in ("mA", "mB"):
                    b = int(n[2:])
                    for g in UNIT_GROUPS[n[:2]]:
                        k = score_bank(ph, "max", b, g)
                        dve.wait_ge(score_full, score_at(ph, "max", b, g))
                        src = score[k][:, 0:HG * KEYS].rearrange("p (h t) -> p h t", h=HG)
                        ve.tensor_reduce(q_st[:, b, HG * g:HG * (g + 1), 3 * HD], src, AX.X, ALU.max,
                                         negate=True).then_inc(score_free[k], 1)
                elif n == "oTT":
                    dve.wait_ge(oh_done, c + 1)
                    ve.tensor_tensor(ol[:, :], mix[:, :], oh[:, :].bitcast(f32), ALU.subtract).then_inc(mix_free, 1)
                elif n[:2] == "oT":
                    b = int(n[2:])
                    dve.wait_ge(mix_full, mix_at(ph, n))
                    o = mix[:, 0:2 * VS].rearrange("p (h s) -> p h s", s=VW)
                    link(c, ve.reciprocal(rden[:, :], o[:, :, HD]))
                    for g in range(2):
                        ins = ve.tensor_tensor(
                            on[:, b, :].rearrange("p (i g j d) -> p i g j d", i=GROUPS, g=2, d=HD)[:, :, g],
                            o[:, g * VG:(g + 1) * VG, 0:HD].rearrange("p (i j) d -> p i j d", j=2),
                            rden[:, g * VG:(g + 1) * VG].rearrange("p (i j) -> p i j", j=2)
                            .unsqueeze(3).to_broadcast([P, GROUPS, 2, HD]), ALU.mult)
                    ins.then_inc(mix_free, 1)
                elif n == "proj":
                    dve.wait_ge(mix_full, mix_at(ph, "proj"))
                    dve.wait_ge(tanh_done, 1)
                    ve.scalar_tensor_tensor(out=x1_chunk(c), in0=mix[:, :], scalar=gates[:, 0:1],
                                            in1=xc[:, :, :].rearrange("p b d -> p (b d)"),
                                            op0=ALU.mult, op1=ALU.add).then_inc(mix_free, 1)
                    dve.wait_ge(mix_free, mix_at(ph, "proj"))
                    hold().then_inc(x1_done, 1)
                elif n == "nrm":
                    moments(c, x1_chunk(c).rearrange("p (b d) -> p b d", b=CB))
                elif n == "ln3":
                    newton(c, *NORM)
                    normed(x1_chunk(c).rearrange("p (b d) -> p b d", b=CB)).then_inc(xn2_done, 1)
                elif n in ("x2T", "gate"):
                    route(ph, n)

            def route(ph, n):
                c = ph.attn
                if n == "x2T":
                    dve.wait_ge(x2h_done, c + 1)
                    ve.tensor_tensor(x2l[:, :], mix[:, :], x2h[:, :].bitcast(f32),
                                     ALU.subtract).then_inc(mix_free, 1)
                elif n == "gate":
                    logits(ph)

            def logits(ph):
                c = ph.attn
                dve.wait_ge(mix_full, mix_at(ph, "gate"))
                ve.tensor_tensor(lg[:, :, :], mix[:, 0:CB * EXPERTS].rearrange("p (b e) -> p b e", b=CB),
                                 bg_sb[:, :].unsqueeze(1).to_broadcast([P, CB, EXPERTS]),
                                 ALU.add).then_inc(mix_free, 1)
                dve.wait_ge(mix_free, mix_at(ph, "gate"))
                link(c, ve.tensor_reduce(r4[:, :], lg[:, :, :], AX.X, ALU.max))
                ve.tensor_tensor(lg[:, :, :], lg[:, :, :], r4[:, :].unsqueeze(2).to_broadcast([P, CB, EXPERTS]),
                                 ALU.subtract).then_inc(lg_done, 1)

            def top_two(ph):
                c = ph.ffn
                dve.wait_ge(ex_done, c + 1)
                link(c, ve.tensor_reduce(s4[:, :], ex[:, :, :], AX.X, ALU.add))
                link(c, ve.reciprocal(r4[:, :], s4[:, :]))
                link(c, ve.tensor_tensor(pr[:, :, :], ex[:, :, :],
                                         r4[:, :].unsqueeze(2).to_broadcast([P, CB, EXPERTS]), ALU.mult))
                hold()
                for b in range(CB):
                    ins = ve.max(top[:, b, :], pr[:, b, :])
                link(c, ins)
                hold()
                for b in range(CB):
                    ins = ve.max_index(topi[:, b, :], top[:, b, :], pr[:, b, :])
                link(c, ins)
                link(c, ve.tensor_copy(topf[:, :, 0:2], topi[:, :, 0:2]))

            def combine(ph):
                c = ph.ffn
                link(c, ve.scalar_tensor_tensor(out=s4[:, :], in0=top[:, :, 0], scalar=TOP_EPS, in1=top[:, :, 1],
                                                op0=ALU.add, op1=ALU.add))
                link(c, ve.reciprocal(r4[:, :], s4[:, :]))
                link(c, ve.tensor_tensor(top[:, :, 0:2], top[:, :, 0:2],
                                         r4[:, :].unsqueeze(2).to_broadcast([P, CB, 2]), ALU.mult))
                io = iota.unsqueeze(1).unsqueeze(1).to_broadcast([P, CB, 2, EXPERTS])
                link(c, ve.tensor_tensor(e12[:, :, :, :], io, topf[:, :, 0:2].unsqueeze(3)
                                         .to_broadcast([P, CB, 2, EXPERTS]), ALU.is_equal))
                link(c, ve.tensor_tensor(e12[:, :, :, :], e12[:, :, :, :], top[:, :, 0:2].unsqueeze(3)
                                         .to_broadcast([P, CB, 2, EXPERTS]), ALU.mult))
                link(c, ve.tensor_tensor(e1[:, :, :], e12[:, :, 0, :], e12[:, :, 1, :], ALU.add))
                link(c, ve.tensor_copy(chi[:, :, :], e1[:, :, :]))
                ve.tensor_copy(c_st[:, :, 0:EXPERTS], chi[:, :, :].bitcast(f32))
                ve.tensor_copy(c_st[:, :, 2 * EXPERTS:3 * EXPERTS], chi[:, :, :].bitcast(f32))
                ve.tensor_tensor(c_st[:, :, EXPERTS:2 * EXPERTS], e1[:, :, :], chi[:, :, :].bitcast(f32),
                                 ALU.subtract).then_inc(cst_done, 1)

            def weigh_y(ph, e):
                c = ph.ffn
                dve.wait_ge(y_part, UNITS * c + FB * (e + 1))
                dve.wait_ge(mix_free, mix_at(ph, f"w{e}"))
                if e == 0:
                    dve.wait_ge(outb_free, c + 1)
                if e >= 2:
                    dve.wait_ge(acc_done, adds(c, e - 1))
                ve.tensor_tensor(yt[:, e % 2, :], y[:, :], cbc[:, e % 2, :], ALU.mult).then_inc(y_free, 1)

            def hidden(c, t):
                dve.wait_ge(gt_full, units(c, t + 1))
                dve.wait_ge(sil_done, units(c, t + 1))
                ve.scalar_tensor_tensor(out=hf[:, t % HB, :], in0=gt[t % 2][:, :], scalar=b3_sb[:, t:t + 1],
                                        in1=hf[:, t % HB, :], op0=ALU.add, op1=ALU.mult).then_inc(h_done, 1)

            def ffn(ph, s):
                if s + LAG < UNITS:
                    if ph.ffn is not None:
                        hidden(ph.ffn, s + LAG)
                elif ph.attn is not None:
                    hidden(ph.attn, s + LAG - UNITS)
                for late in (0, 1):
                    for n in due(ph, "dve", s, late):
                        if n == "top":
                            top_two(ph)
                        elif n == "comb":
                            combine(ph)
                        elif n in SIDE:
                            weigh_y(ph, int(n[1:]))
                        else:
                            attn(ph, n)

            def finish(ph):
                c = ph.ffn
                weigh_y(ph, EXPERTS - 1)
                dve.wait_ge(mix_full, mix_at(ph, "fin"))
                ve.scalar_tensor_tensor(out=outb, in0=mix[:, :], scalar=gates[:, 1:2], in1=x1_chunk(c),
                                        op0=ALU.mult, op1=ALU.add).then_inc(mix_free, 1)

            dve.wait_ge(init_done, 3)
            ph = enter(start_phase())
            for n in first_steps("dve", True):
                if n == "ln1":
                    small_parts()
                attn(ph, n)
            assert links[0] == FRONT_LINKS, links[0]
            biases()
            ph = enter(first_phase())
            for n in first_steps("dve", False):
                attn(ph, n)
            for s in range(FRONT_SLOT, UNITS):
                ffn(ph, s)
            assert links[0] == FRONT_LINKS + REST_LINKS, links[0]
            with dve.Fori(0, CHUNKS - 2) as i:
                ph = enter(middle_phase(i))
                for s in range(UNITS):
                    ffn(ph, s)
                finish(ph)
                assert links[0] == LINKS, links[0]
            for ph in (late_phase(), last_phase()):
                enter(ph)
                for s in range(UNITS):
                    ffn(ph, s)
                finish(ph)

        @block.tensor
        def _(pe):
            pe.wait_ge(cst_in, 16)

            def three(dst, a_hi, a_lo, b_hi, b_lo, start=True, stop=True):
                nc.tensor.matmul(dst, a_hi, b_hi, start=start, stop=False)
                nc.tensor.matmul(dst, a_lo, b_hi, start=False, stop=False)
                return nc.tensor.matmul(dst, a_hi, b_lo, start=False, stop=stop)

            def turn(dst, src, n):
                return nc.tensor.transpose(dst, src, ident[0:n, 0:n])

            def attn(ph, n):
                c = chunk_of(ph, n)
                if n[:-1] in UNIT_GROUPS:
                    kind, b = "max" if n[0] == "m" else "sc", int(n[-1])
                    if kind == "max":
                        pe.wait_ge(kbd_done, CB * c + b + 1)
                    if n[:2] == "sA":
                        pe.wait_ge(mix_free, mix_at(ph, f"qS{b}"))
                    for g in UNIT_GROUPS[n[:-1]]:
                        k = score_bank(ph, kind, b, g)
                        pe.wait_ge(score_free[k], score_before(ph, kind, b, g))
                        r = slice(SLOT * g, SLOT * (g + 1))
                        if kind == "max":
                            last = nc.tensor.matmul(score[k][:, 0:HG * KEYS], qTh[r, b * P:(b + 1) * P],
                                                    k_bd[r, b, :, :].rearrange("p h t -> p (h t)"),
                                                    start=True, stop=True)
                        else:
                            for i in range(GROUPS):
                                last = nc.tensor.matmul(score[k][0:KEYS, i * P:(i + 1) * P],
                                                        ksT[r, b, i, :], qsT[r, b % 2, i, :],
                                                        start=True, stop=True)
                        last.then_inc(score_full, 1)
                    return
                if n[:4] == "warm":
                    for _ in range(4 * int(n[4:])):
                        nc.tensor.matmul(y[:, 0:KVW], wkv[:, 0, 0:P], wkv[:, 0, :], start=True, stop=True)
                    return
                if n == "xT":
                    pe.wait_ge(xn_done, c + 1)
                elif n == "cT":
                    pe.wait_ge(c_in, 16 * c + 16)
                elif n == "kT":
                    pe.wait_ge(kn_done, c + 1)
                elif n == "qT":
                    pe.wait_ge(qn_done, c + 1)
                elif n[:2] == "kS":
                    pe.wait_ge(kdup_done, 2 * CB * c + 2 * (int(n[2:]) + 1))
                    pe.wait_ge(klo_done, CB * c + int(n[2:]) + 1)
                elif n[:2] == "qS":
                    b = int(n[2:])
                    pe.wait_ge(qdup_done, 2 * CB * c + 2 * (b + 1))
                    for g in (2, 3):
                        pe.wait_ge(score_free[score_bank(ph, "max", b, g)], score_before(ph, "max", b, g) + 1)
                elif n[:2] == "pv":
                    b = int(n[2:])
                    for g in (2, 3):
                        pe.wait_ge(score_free[score_bank(ph, "sc", b, g)], score_before(ph, "sc", b, g) + 1)
                    pe.wait_ge(va_done, 2 * CB * c + 2 * (b + 1))
                elif n == "x2T":
                    pe.wait_ge(xn2_done, c + 1)
                pe.wait_ge(mix_free, mix_before(ph, n))
                if n == "xT":
                    for b in range(CB):
                        last = turn(mix[:, b * P:(b + 1) * P], xn[:, b, :], P)
                elif n == "q":
                    for b in range(CB):
                        s = slice(b * P, (b + 1) * P)
                        last = three(mix[:, s], xh[:, s], xl[:, s], wq[:, 0, :], wq[:, 1, :])
                elif n == "cT":
                    for b in range(CB):
                        last = turn(mix[:, b * KEYS:(b + 1) * KEYS], cc[:, b, :], KEYS)
                elif n[:2] == "kv":
                    for k in range(2):
                        s = slice((2 * int(n[2:]) + k) * KEYS, (2 * int(n[2:]) + k + 1) * KEYS)
                        last = three(mix[0:KEYS, k * KVW:(k + 1) * KVW], ch[:, s], cl[:, s],
                                     wkv[:, 0, :], wkv[:, 1, :])
                elif n == "qT":
                    for b in range(CB):
                        last = turn(mix[:, b * P:(b + 1) * P], qn[:, b * D:(b + 1) * D], P)
                elif n == "kT":
                    for b in range(CB):
                        last = turn(mix[:, b * KEYS:(b + 1) * KEYS], kn[:, b * D:(b + 1) * D], KEYS)
                elif n[:2] == "kS":
                    for i in range(GROUPS):
                        src = k_st[:, int(n[2:]), HG * i:HG * (i + 1), :].rearrange("p h s -> p (h s)")
                        last = turn(mix[:, i * KEYS:(i + 1) * KEYS], src, KEYS)
                elif n[:2] == "qS":
                    for i in range(GROUPS):
                        src = q_st[:, int(n[2:]), HG * i:HG * (i + 1), :].rearrange("p h s -> p (h s)")
                        last = turn(mix[:, i * P:(i + 1) * P], src, P)
                elif n[:2] == "pv":
                    b = int(n[2:])
                    for g in range(2):
                        for h in range(VG):
                            i, j = h // 2, 2 * g + h % 2
                            last = nc.tensor.matmul(mix[0:VS, g * P:(g + 1) * P],
                                                    va[:, g, h * VS:(h + 1) * VS],
                                                    probs[:, j, i, :], start=(h == 0), stop=(h == VG - 1))
                        if g == 0:
                            last.then_inc(pv_half, 1)
                elif n == "oTT":
                    for b in range(CB):
                        last = turn(mix[:, b * P:(b + 1) * P], on[:, b, :], P)
                elif n[:2] == "oT":
                    for g in range(2):
                        last = turn(mix[:, g * VS:(g + 1) * VS], oa[:, g * P:(g + 1) * P], VS)
                elif n == "proj":
                    for b in range(CB):
                        s = slice(b * P, (b + 1) * P)
                        last = three(mix[:, s], oh[:, s], ol[:, s], wp[:, 0, :], wp[:, 1, :])
                elif n == "x2T":
                    for b in range(CB):
                        last = turn(mix[:, b * P:(b + 1) * P], xn[:, b, :], P)
                elif n == "gate":
                    for b in range(CB):
                        s = slice(b * P, (b + 1) * P)
                        last = three(mix[:, b * EXPERTS:(b + 1) * EXPERTS], x2h[:, s], x2l[:, s],
                                     wg[:, 0, :], wg[:, 1, :])
                last.then_inc(mix_full, 1)

            def side(ph, n):
                if n == "wT":
                    pe.wait_ge(cst_done, ph.ffn + 1)
                if n == "fin":
                    pe.wait_ge(acc_done, adds(ph.ffn, EXPERTS - 1))
                pe.wait_ge(mix_free, mix_before(ph, n))
                if n == "fin":
                    for b in range(CB):
                        s = slice(b * P, (b + 1) * P)
                        nc.tensor.matmul(mix[:, s], acc[:, s], ident, start=(b == 0), stop=False)
                    pe.wait_ge(y_free, y_reads(ph.ffn, EXPERTS))
                    for b in range(CB):
                        s = slice(b * P, (b + 1) * P)
                        ins = nc.tensor.matmul(mix[:, s], yt[:, (EXPERTS - 1) % 2, s], ident,
                                               start=False, stop=(b == CB - 1))
                elif n == "wT":
                    for b in range(CB):
                        ins = turn(mix[0:SLOT, b * P:(b + 1) * P], c_st[:, b, :], P)
                elif n == "b2":
                    pe.wait_ge(gk_done, 4)
                    ins = nc.tensor.matmul(mix[:, :], b2_s[:, :], cT[0:WR, :], start=True, stop=True)
                else:
                    e = int(n[1:])
                    ins = nc.tensor.matmul(mix[:, :], sel[0:16, e:e + 1].to_broadcast([16, P]), cT[0:16, :],
                                           start=True, stop=True)
                ins.then_inc(mix_full, 1)

            def hidden(c, t, fresh=False):
                e, f = divmod(t, FB)
                for k, (bank_, full, free) in enumerate([(up[t % 2], up_full, sil_done),
                                                         (gt[t % 2], gt_full, h_done)]):
                    if not fresh or t >= 2:
                        pe.wait_ge(free, units(c, t - 1))
                    s = slice(k * FF + f * P, k * FF + (f + 1) * P)
                    three(bank_[:, :], w_hi[:, e, s], w_lo[:, e, s], x2h[:, :], x2l[:, :]).then_inc(full, 1)

            def down(ph, t):
                c, (e, f) = ph.ffn, divmod(t, FB)
                pe.wait_ge(hl_done, units(c, t + 1))
                if f == 0:
                    pe.wait_ge(y_free, y_reads(c, e))
                s = slice(2 * FF + f * P, 2 * FF + (f + 1) * P)
                three(y[:, :], w_hi[:, e, s], w_lo[:, e, s], hh[:, t % PB, :], hl[:, t % PB, :],
                      start=(f == 0), stop=(f == FB - 1)).then_inc(y_part, 1)

            def ffn(ph, s):
                if s + LAG < UNITS:
                    if ph.ffn is not None:
                        hidden(ph.ffn, s + LAG)
                elif ph.attn is not None:
                    if s + LAG == UNITS:
                        pe.wait_ge(mix_free, mix_at(ph, "x2T"))
                    hidden(ph.attn, s + LAG - UNITS, fresh=ph.ffn is None)
                for late in (0, 1):
                    if late and ph.ffn is not None:
                        down(ph, s)
                    for n in due(ph, "pe", s, late):
                        (side if n in SIDE else attn)(ph, n)

            for n in first_steps("pe", True):
                if n == "kv0":
                    pe.wait_ge(small_hi, 5)
                    pe.wait_ge(small_lo, 4)
                attn(start_phase(), n)
            ph = first_phase()
            for n in first_steps("pe", False):
                attn(ph, n)
            pe.wait_ge(w_lo_done, EXPERTS)
            for s in range(FRONT_SLOT, UNITS):
                ffn(ph, s)
            with pe.Fori(0, CHUNKS - 2) as i:
                ph = middle_phase(i)
                for s in range(UNITS):
                    ffn(ph, s)
            for ph in (late_phase(), last_phase()):
                for s in range(UNITS):
                    ffn(ph, s)


def kernel(**inputs):
    import numpy as np
    import concourse.bacc as bacc
    from concourse.bass_utils import run_bass_kernel_spmd

    def blocks(a):
        return a.reshape(EXPERTS, FB, P).transpose(2, 0, 1).reshape(P, UNITS)

    sel = np.zeros((P, EXPERTS), np.float32)
    for e in range(EXPERTS):
        sel[e, e] = 1
        sel[e + EXPERTS, e] = 1
    consts = np.concatenate([
        np.eye(P, dtype=np.float32),
        (np.arange(P)[:, None] // HD % HG == np.arange(HG)[None, :]).astype(np.float32),
        np.tile(np.arange(EXPERTS, dtype=np.float32), (P, 1)),
        (np.arange(P)[:, None] < 2 * EXPERTS).astype(np.float32),
        (np.arange(P)[:, None] >= 2 * EXPERTS).astype(np.float32),
        sel], axis=1)
    laid = {n: np.ascontiguousarray(a) for n, a in inputs.items()}
    laid["L0_ffn_b1"] = np.ascontiguousarray(blocks(laid["L0_ffn_b1"]))
    laid["L0_ffn_b3"] = np.ascontiguousarray(blocks(laid["L0_ffn_b3"]))
    laid["consts"] = consts
    names = ['x', 'ctx_1024', 'g_xattn', 'g_ffn', 'L0_xattn_Wq', 'L0_xattn_Wkv', 'L0_xattn_Wproj',
             'L0_xattn_q_gamma', 'L0_xattn_k_gamma', 'L0_ffn_Wg', 'L0_ffn_bg', 'L0_ffn_W1', 'L0_ffn_b1',
             'L0_ffn_W3', 'L0_ffn_b3', 'L0_ffn_W2', 'L0_ffn_b2', 'consts']
    nc = bacc.Bacc("TRN2", target_bir_lowering=False, num_devices=1)
    f32 = mybir.dt.float32
    arrays = {f"in_{n}": laid[n] for n in names}
    args = [nc.dram_tensor(f"in_{n}", laid[n].shape, f32, kind="ExternalInput").ap() for n in names]
    out = nc.dram_tensor("out_x", (NBATCH, P, D), f32, kind="ExternalOutput").ap()
    build(nc, *args, out)
    r = run_bass_kernel_spmd(nc, [arrays], core_ids=[0])
    return r.results[0]["out_x"]
```
